# Optimizing a Trainium2 kernel written in Bass

```python
import numpy as np
import jax
import jax.numpy as jnp

def _softmax(x, axis=-1):
    return jax.nn.softmax(x, axis=axis)

def _gelu(x):
    return jax.nn.gelu(x, approximate=True)

def _silu(x):
    return jax.nn.silu(x)

def _sigmoid(x):
    return jax.nn.sigmoid(x)

def _layernorm(x, axis=-1, eps=1e-05):
    m = jnp.mean(x, axis=axis, keepdims=True)
    v = jnp.var(x, axis=axis, keepdims=True)
    return (x - m) / jnp.sqrt(v + eps)

def _scatter_add(tgt, idx, src, axis=0):
    return tgt.at[idx].add(src)

def _segment_sum(src, seg, n):
    return jax.ops.segment_sum(src, seg, n)
kernel_name = 'mk_gnn_resnorm_d2_gnn_r32_c1112f'

def setup_inputs(seed: int=0):
    np.random.seed(seed)
    _w = jnp.asarray

    def _rec_inputs():
        import jax
        import jax.numpy as jnp
        _gk = jax.random.key(seed)
        x = -0.0003713 + 1 * jax.random.normal(jax.random.fold_in(_gk, 1), (3125, 128), jnp.float32)
        src = jax.random.randint(jax.random.fold_in(_gk, 2), (100000,), 0, 3125, jnp.int32)
        dst = jax.random.randint(jax.random.fold_in(_gk, 3), (100000,), 0, 3125, jnp.int32)
        _o = jnp.argsort(dst, stable=True)
        src = src[_o]
        dst = dst[_o]
        edge_type_8 = jax.random.randint(jax.random.fold_in(_gk, 13), (100000,), 0, 8, jnp.int32)
        return (x, src, dst, edge_type_8)
    x, src, dst, edge_type_8 = _rec_inputs()

    def _L0_gnn_setup():
        import jax, jax.numpy as jnp
        import numpy as np
        NEG_SLOPE = 0.2
        EPS = 1e-16
        N_NODES = 3125
        N_EDGES = 50000
        D = 128
        H = 4
        C = 32
        L = 3

        def _gat_layer(h, src, dst, Ws, Wd, a_s, a_d, bias):
            N = h.shape[0]
            xs = (h @ Ws).reshape(N, H, C)
            xd = (h @ Wd).reshape(N, H, C)
            alpha_s = jnp.sum(xs * a_s, axis=-1)
            alpha_d = jnp.sum(xd * a_d, axis=-1)
            e = alpha_s[src] + alpha_d[dst]
            e = jax.nn.leaky_relu(e, NEG_SLOPE)
            emax = jax.ops.segment_max(e, dst, num_segments=N)
            ex = jnp.exp(e - emax[dst])
            denom = jax.ops.segment_sum(ex, dst, num_segments=N)
            alpha = ex / (denom[dst] + EPS)
            msg = xs[src] * alpha[:, :, None]
            out = jax.ops.segment_sum(msg, dst, num_segments=N)
            return out.reshape(N, H * C) + bias
        key = jax.random.key(seed)
        ks = jax.random.split(key, 7)
        x = jax.random.normal(ks[0], (N_NODES, D), dtype=jnp.float32)
        edge_index = jax.random.randint(ks[1], (2, N_EDGES), 0, N_NODES, dtype=jnp.int32)
        scale = 1.0 / np.sqrt(D)
        Ws = jax.random.normal(ks[2], (L, D, H * C), dtype=jnp.float32) * scale
        Wd = jax.random.normal(ks[3], (L, D, H * C), dtype=jnp.float32) * scale
        att_s = jax.random.normal(ks[4], (L, H, C), dtype=jnp.float32) * scale
        att_d = jax.random.normal(ks[5], (L, H, C), dtype=jnp.float32) * scale
        b = jnp.zeros((L, H * C), dtype=jnp.float32)
        return {'x': x, 'edge_index': edge_index, 'Ws': Ws, 'Wd': Wd, 'att_s': att_s, 'att_d': att_d, 'b': b}
    _L0_gnn_all = _L0_gnn_setup()
    _L0_gnn_in = {k: v for k, v in _L0_gnn_all.items() if k in ('Ws', 'Wd', 'att_s', 'att_d', 'b')}
    del _L0_gnn_all

    def _L1_gnn_setup():
        import jax, jax.numpy as jnp
        import numpy as np
        N_NODES = 50000
        N_EDGES = 18750
        IN_FEAT = 128
        OUT_FEAT = 128
        NUM_RELS = 8
        key = jax.random.key(seed)
        ks = jax.random.split(key, 9)
        return {'h': jax.random.normal(ks[0], (N_NODES, IN_FEAT), dtype=jnp.float32), 'W': jax.random.normal(ks[1], (NUM_RELS, IN_FEAT, OUT_FEAT), dtype=jnp.float32) * 0.05, 'bias_term': jax.random.normal(ks[2], (NUM_RELS, OUT_FEAT), dtype=jnp.float32) * 0.05, 'gate_weight': jax.random.normal(ks[3], (NUM_RELS, OUT_FEAT, 1), dtype=jnp.float32) * 0.05, 'gate_bias': jax.random.normal(ks[4], (NUM_RELS, 1), dtype=jnp.float32) * 0.05, 'loop_weight': jax.random.normal(ks[5], (IN_FEAT, OUT_FEAT), dtype=jnp.float32) * 0.05, 'src': jax.random.randint(ks[6], (N_EDGES,), 0, N_NODES, dtype=jnp.int32), 'dst': jax.random.randint(ks[7], (N_EDGES,), 0, N_NODES, dtype=jnp.int32), 'rel': jax.random.randint(ks[8], (N_EDGES,), 0, NUM_RELS, dtype=jnp.int32)}
    _L1_gnn_all = _L1_gnn_setup()
    _L1_gnn_in = {k: v for k, v in _L1_gnn_all.items() if k in ('W', 'bias_term', 'gate_weight', 'gate_bias', 'loop_weight')}
    del _L1_gnn_all
    return {'x': x, 'src': src, 'dst': dst, 'edge_type_8': edge_type_8, 'L0_gnn_Ws': _L0_gnn_in['Ws'], 'L0_gnn_Wd': _L0_gnn_in['Wd'], 'L0_gnn_att_s': _L0_gnn_in['att_s'], 'L0_gnn_att_d': _L0_gnn_in['att_d'], 'L0_gnn_b': _L0_gnn_in['b'], 'L1_gnn_W': _L1_gnn_in['W'], 'L1_gnn_bias_term': _L1_gnn_in['bias_term'], 'L1_gnn_gate_weight': _L1_gnn_in['gate_weight'], 'L1_gnn_gate_bias': _L1_gnn_in['gate_bias'], 'L1_gnn_loop_weight': _L1_gnn_in['loop_weight']}

def reference(x, src, dst, edge_type_8, L0_gnn_Ws, L0_gnn_Wd, L0_gnn_att_s, L0_gnn_att_d, L0_gnn_b, L1_gnn_W, L1_gnn_bias_term, L1_gnn_gate_weight, L1_gnn_gate_bias, L1_gnn_loop_weight):
    import jax
    import jax.numpy as jnp

    def _L0_gnn_ref(x, edge_index, Ws, Wd, att_s, att_d, b):
        import jax, jax.numpy as jnp
        import numpy as np
        NEG_SLOPE = 0.2
        EPS = 1e-16
        N_NODES = 3125
        N_EDGES = 50000
        D = 128
        H = 4
        C = 32
        L = 3

        def _gat_layer(h, src, dst, Ws, Wd, a_s, a_d, bias):
            N = h.shape[0]
            xs = (h @ Ws).reshape(N, H, C)
            xd = (h @ Wd).reshape(N, H, C)
            alpha_s = jnp.sum(xs * a_s, axis=-1)
            alpha_d = jnp.sum(xd * a_d, axis=-1)
            e = alpha_s[src] + alpha_d[dst]
            e = jax.nn.leaky_relu(e, NEG_SLOPE)
            emax = jax.ops.segment_max(e, dst, num_segments=N)
            ex = jnp.exp(e - emax[dst])
            denom = jax.ops.segment_sum(ex, dst, num_segments=N)
            alpha = ex / (denom[dst] + EPS)
            msg = xs[src] * alpha[:, :, None]
            out = jax.ops.segment_sum(msg, dst, num_segments=N)
            return out.reshape(N, H * C) + bias
        src = edge_index[0]
        dst = edge_index[1]
        h = x
        for i in range(L):
            h = _gat_layer(h, src, dst, Ws[i], Wd[i], att_s[i], att_d[i], b[i])
            if i < L - 1:
                h = jax.nn.relu(h)
        return h

    def _L1_gnn_ref(h, W, bias_term, gate_weight, gate_bias, loop_weight, src, dst, rel):
        import jax, jax.numpy as jnp
        import numpy as np
        N_NODES = 50000
        N_EDGES = 18750
        IN_FEAT = 128
        OUT_FEAT = 128
        NUM_RELS = 8
        n_nodes = h.shape[0]
        loop_message = h @ loop_weight
        xw = jnp.einsum('ni,rio->rno', h, W)
        msg = xw[rel, src] + bias_term[rel]
        gw = gate_weight[..., 0]
        gate = jax.nn.sigmoid(jnp.sum(msg * gw[rel], axis=-1) + gate_bias[rel, 0])
        agg = jax.ops.segment_sum(msg * gate[:, None], dst, num_segments=n_nodes)
        node_repr = agg + loop_message
        return jax.nn.relu(node_repr)
    edge_index = jnp.stack([src, dst])
    x = _layernorm(x + _L0_gnn_ref(x, edge_index, L0_gnn_Ws, L0_gnn_Wd, L0_gnn_att_s, L0_gnn_att_d, L0_gnn_b), axis=-1)
    x = _layernorm(x + _L1_gnn_ref(x, L1_gnn_W, L1_gnn_bias_term, L1_gnn_gate_weight, L1_gnn_gate_bias, L1_gnn_loop_weight, src, dst, edge_type_8), axis=-1)
    return x

_drawn_inputs = setup_inputs


def setup_inputs(seed=0):
    import zlib

    import numpy as np

    out = dict(_drawn_inputs(seed))
    spreads = {'L0_gnn_b': (0.0, 0.1)}
    factors = {}
    for name, (base, spread) in spreads.items():
        noise = np.random.default_rng([zlib.crc32(name.encode()), seed]).standard_normal(out[name].shape)
        drawn = base * np.exp(spread * noise) if base else spread * noise
        out[name] = jnp.asarray(drawn.astype(out[name].dtype))
    for name, factor in factors.items():
        out[name] = (out[name] * factor).astype(out[name].dtype)
    return out
```

```python
from contextlib import ExitStack

import concourse.bass as bass
from concourse import mybir

F32 = mybir.dt.float32
I32 = mybir.dt.int32
ALU = mybir.AluOpType
ACT = mybir.ActivationFunctionType
AX = mybir.AxisListType.X
ENG = mybir.EngineType

P = 128
N = 3125
E = 100000
D = 128
H = 4
C = D // H
L = 3
NREL = 8
SLOPE = 0.2
EPS_DEN = 1e-16
EPS_LN = 1e-5

W = P // H
J = 4
GE = J * P
GR = 98
G = 2 * GR
NT = (N + P - 1) // P
NP = NT * P
U = 8
LAG = 2
LAG_SUM = 3
LAG_ADD = 4
NW = NP // W
PAD_DST = (N + W - 1) // W * W - 1
NWX = PAD_DST // W + U
RING = 14
ITS = G // RING
HALF = RING // 2
LAG_FREE = 10
RW = D + 1 + H
AW = D + 1
SHRINK = 2.0 ** -64
FLOOR = 1e15
VB = 512
VMAX = G * (N // W + 1) + 2 * VB
assert RING * ITS == G and PAD_DST < NP and NWX >= NW


def build(nc, x, src, dst, et, Ws, Wd, att_s, att_d, gat_b, Wr, rel_b, gate_w, gate_b, loop_w, out):
    with ExitStack() as ctx:
        def sb(name, shape, dt=F32):
            return ctx.enter_context(nc.sbuf_tensor(name, shape, dt))

        def sem(name):
            return ctx.enter_context(nc.semaphore(name))

        xtab = nc.dram_tensor("xtab", (NP, RW), F32).ap()
        gtab = nc.dram_tensor("gtab", (NP * NREL, D), F32).ap()
        vis = nc.dram_tensor("vis", (VMAX,), I32).ap()

        ident = sb("ident", [P, P])
        eye_w = sb("eye_w", [P, W])
        node_no = sb("node_no", [P, NWX * W])
        x_nm = sb("x_nm", [P, NT, D])
        h_fm = sb("h_fm", [P, NP])
        acc = sb("acc", [P, NWX * AW])
        ring = sb("ring", [P, RING, J, RW])
        stage = sb("stage", [P, NT, RW])
        dst_e = sb("dst_e", [P, G, J])
        idx_gat = sb("idx_gat", [P, G * J], I32)
        idx_rel = sb("idx_rel", [P, G * J], I32)
        idx_now = sb("idx_now", [P, 2, HALF * J], I32)
        w_gat = sb("w_gat", [P, L, D + H])
        w_now = sb("w_now", [P, D + H])
        wd_sb = sb("wd_sb", [P, L, D])
        ad_w = sb("ad_w", [P, L, H])
        adx_now = sb("adx_now", [P, H, W])
        bias_gat = sb("bias_gat", [P, L])
        relu_floor = sb("relu_floor", [P, L])
        att_bc = sb("att_bc", [P, 2, L, D])
        ad4 = sb("ad4", [P, NWX])
        nmax = sb("nmax", [P, NWX])
        rden = sb("rden", [P, NW])
        dist = sb("dist", [P, 2, J, W])
        lmask = sb("lmask", [P, 2, J, P])
        relu4 = sb("relu4", [P, 2, GE])
        nz = sb("nz", [P, 2, GE])
        nmax_old = sb("nmax_old", [P, U])
        nmax_new = sb("nmax_new", [P, 2])
        pt = sb("pt", [P, 2, GE])
        fade = sb("fade", [P, U])
        pe_w = sb("pe_w", [P, 2, J, P])
        wr_sb = sb("wr_sb", [P, NREL, D])
        relb_bc = sb("relb_bc", [P, NREL * D])
        gw_bc = sb("gw_bc", [P, NREL * D])
        gateb_bc = sb("gateb_bc", [P, NREL])
        wg = sb("wg", [P, NREL])
        gbias = sb("gbias", [P, NREL])
        gz = sb("gz", [P, 2, NREL])
        ge = sb("ge", [P, 2, NREL])
        gate = sb("gate", [P, 2, NREL])
        loop_sb = sb("loop_sb", [P, D])
        bn6 = sb("bn6", [P, NT, 6])
        mv = sb("mv", [P, NT, 2])
        rstd = sb("rstd", [P, NT])
        vcode = sb("vcode", [P, J], I32)
        vnum = sb("vnum", [P, J])
        ctl_f = sb("ctl_f", [1, 1])
        ctl = sb("ctl", [1, 4], I32)
        incl_i = sb("incl_i", [1, G], I32)

        acc_w = acc[:].rearrange("p (w c) -> p w c", c=AW)
        ring_flat = ring[:].rearrange("p r j c -> p (r j c)")
        acc_w = acc_w[:, 0:NW, :]
        diag = ring_flat[:, 0:NP]
        diag_t = ring_flat[:, NP:2 * NP]
        msg = ring_flat[:, 0:2 * NREL * D].rearrange("p (b m) -> p b m", b=2)
        gmsg = ring_flat[:, 2 * NREL * D:4 * NREL * D].rearrange("p (b m) -> p b m", b=2)
        rows_i = [acc[0:GR, k * 1024:(k + 1) * 1024].bitcast(I32).rearrange("p (r e) -> p r e", r=2)
                  for k in range(3)]
        rows_f = [acc[0:GR, (3 + k) * 1024:(4 + k) * 1024].rearrange("p (r e) -> p r e", r=2)
                  for k in range(3)]
        mm = acc[0:GR, 6144:6148]
        mmi = acc[0:GR, 6148:6152].bitcast(I32)
        lo_cnt = acc[0:GR, 6152:6156]
        lo_cnt_x = acc[0:GR, 6156:6156 + 4 * P].rearrange("p (k m) -> p k m", k=4)
        vrow = acc[:, 6700:6700 + 6 * G].rearrange("p (k g) -> p k g", k=6)
        ones_g, incl, off, gap, step_k, lead = (vrow[:, k, :] for k in range(6))
        vge = acc[:, 8000:8000 + J * G].rearrange("p (q g) -> p q g", q=J)
        vwt = acc[:, 8800:8800 + J * G].rearrange("p (q g) -> p q g", q=J)
        fold = acc[:, 9600:9600 + NREL * D]
        vsum = acc[:, 10700:10700 + J]

        ps = [ctx.enter_context(nc.psum_tensor(f"bank{i}", [P, 512], F32)) for i in range(8)]
        ps_scores, ps_w, ps_sum, ps_x = ps[0:2], ps[2:4], ps[4:6], ps[6:8]

        s_const = sem("s_const")
        s_w = sem("s_w")
        s_xin = sem("s_xin")
        s_edge = sem("s_edge")
        s_pad = sem("s_pad")
        s_rows = sem("s_rows")
        s_set = sem("s_set")
        s_setf = sem("s_setf")
        s_lc = sem("s_lc")
        s_ctl = sem("s_ctl")
        s_code = sem("s_code")
        s_vis = sem("s_vis")
        s_ready = sem("s_ready")
        s_now = sem("s_now")
        s_h = sem("s_h")
        s_t = sem("s_t")
        s_tu = sem("s_tu")
        s_ad = sem("s_ad")
        s_adu = sem("s_adu")
        s_tab = sem("s_tab")
        s_zero = sem("s_zero")
        s_idx = sem("s_idx")
        s_row = [sem(f"s_row{k}") for k in range(RING)]
        s_landed = sem("s_landed")
        s_free = sem("s_free")
        s_p = sem("s_p")
        s_pt = sem("s_pt")
        s_pc = sem("s_pc")
        s_sum = sem("s_sum")
        s_added = sem("s_added")
        s_mask = sem("s_mask")
        s_sc = sem("s_sc")
        s_relu = sem("s_relu")
        s_max = sem("s_max")
        s_n = sem("s_n")
        s_nu = sem("s_nu")
        s_var = sem("s_var")
        s_root = sem("s_root")
        s_norm = sem("s_norm")
        s_x1 = sem("s_x1")
        s_x1u = sem("s_x1u")
        s_m = sem("s_m")
        s_mu = sem("s_mu")
        s_gz = sem("s_gz")
        s_ge = sem("s_ge")
        s_gate = sem("s_gate")
        s_gm = sem("s_gm")
        s_gt = [sem(f"s_gt{b}") for b in range(2)]
        s_stood = sem("s_stood")
        s_out = sem("s_out")

        block = ctx.enter_context(nc.Block())
        edge_lists = (dst, src, et)
        full_rows = E // GE - GR
        tail = E - (GR + full_rows) * GE

        def stand(eng, s, value):
            eng.wait_ge(s, value)
            eng.sem_inc(s_stood, 1)

        def counts(eng):
            eng.wait_ge(s_ctl, 1)
            n_bodies = eng.value_load(ctl[0:1, 0:1], min_val=G // U, max_val=VMAX // U)
            n_visits = eng.value_load(ctl[0:1, 1:2], min_val=G, max_val=VMAX)
            tail = eng.value_load(ctl[0:1, 3:4], min_val=G - U, max_val=VMAX - 2 * U)
            return n_bodies, n_visits, tail

        def codes(eng, kind, first, n):
            _, got = nc.values_load_multi_w_load_instructions(
                vis[bass.ds(first, n)].rearrange("(a b) -> a b", a=1), engines=[kind], min_val=0,
                max_val=(RING << 15) - 1, skip_runtime_bounds_check_because="made on chip from slot, group and window")
            return got

        MADE = "the codes are made on chip from slot, group and window numbers"

        def slot_of(eng, code):
            return nc.s_assert_within(code >> 15, 0, RING - 1, skip_runtime_bounds_check_because=MADE)

        def group_of(eng, code):
            return nc.s_assert_within((code >> 7) & 255, 0, G - 1, skip_runtime_bounds_check_because=MADE)

        def window_of(eng, code):
            return nc.s_assert_within(code & 127, 0, NWX - 1, skip_runtime_bounds_check_because=MADE)

        @block.sync
        def _(sp):
            for k, a in enumerate(edge_lists):
                sp.dma_start(rows_i[k][:, 0, :], a[0:GR * GE].rearrange("(p e) -> p e", e=GE)).then_inc(s_edge, 16)
            sp.wait_ge(s_pad, 1)
            for k, a in enumerate(edge_lists):
                sp.dma_start(rows_i[k][0:full_rows, 1, :],
                             a[GR * GE:(GR + full_rows) * GE].rearrange("(p e) -> p e", e=GE)).then_inc(s_edge, 16)
                sp.dma_start(rows_i[k][full_rows:GR, 1, 0:tail],
                             a[(GR + full_rows) * GE:E].rearrange("(p e) -> p e", p=1)).then_inc(s_edge, 16)
            nf = N // P
            sp.dma_start(x_nm[:, 0:nf, :], x[0:nf * P, :].rearrange("(t p) d -> p t d", p=P)).then_inc(s_xin, 16)
            sp.dma_start(x_nm[0:N - nf * P, nf, :], x[nf * P:N, :]).then_inc(s_xin, 16)
            sp.wait_ge(s_ctl, 1)
            n_blocks = sp.value_load(ctl[0:1, 2:3], min_val=1, max_val=VMAX // VB)
            _, n_visits, _ = counts(sp)
            with sp.Fori(0, n_blocks) as b:
                sp.wait_ge(s_code, b + 1)
                sp.dma_start(vis[bass.ds(b * VB, VB)].rearrange("(p q) -> p q", q=J), vcode[:]).then_inc(s_vis, 16)

            sp.sem_inc(s_free, RING)

            def follow(base, landed0, its0):
                def landed(it, k):
                    sp.wait_ge(s_row[k], (it + its0 + 1) * (16 * J))
                    sp.sem_inc(s_landed, 1)

                def free(g):
                    last = sp.value_load(incl_i[0:1, bass.ds(g, 1)], min_val=1, max_val=VMAX)
                    sp.wait_ge(s_sum, base + last + LAG_ADD)
                    sp.sem_inc(s_free, 1)

                for k in range(RING):
                    landed(0, k)
                    if k >= LAG_FREE:
                        free(k - LAG_FREE)
                with sp.Fori(1, ITS) as it:
                    for k in range(RING):
                        landed(it, k)
                        free(it * RING + (k - LAG_FREE))
                for g in range(G - LAG_FREE, G):
                    free(g)

            with sp.Fori(0, L) as l:
                part = NT // 5
                for m in range(5):
                    sp.wait_ge(s_tu, l * NT + part * (m + 1))
                    sp.dma_start(xtab[m * part * P:(m + 1) * part * P, :].rearrange("(t p) c -> p t c", p=P),
                                 stage[:, m * part:(m + 1) * part, :]).then_inc(s_tab, 16)
                follow(l * n_visits, l * G, l * ITS)
            for t in range(NT):
                sp.wait_ge(s_gm, t + 1)
                sp.dma_start(gtab[t * P * NREL:(t + 1) * P * NREL, :].rearrange("(p r) d -> p (r d)", r=NREL),
                             gmsg[:, t % 2, :]).then_inc(s_gt[t % 2], 16)
            follow(n_visits * L, L * G, L * ITS)
            for t0 in range(0, nf, 6):
                t1 = min(t0 + 6, nf)
                sp.wait_ge(s_norm, NT + t1)
                sp.dma_start(out[t0 * P:t1 * P, :].rearrange("(t p) d -> p t d", p=P), x_nm[:, t0:t1, :]).then_inc(s_out, 16)
            sp.wait_ge(s_norm, 2 * NT)
            sp.dma_start(out[nf * P:N, :], x_nm[0:N - nf * P, nf, :]).then_inc(s_out, 16)
            sp.wait_ge(s_out, 16 * ((nf + 5) // 6 + 1))

        @block.gpsimd
        def _(pool):
            pool.memset(ident[:], 0.0).then_inc(s_const, 1)
            pool.wait_ge(s_const, 1)
            pool.affine_select(ident[:], ident[:], [[-1, P]], ALU.not_equal, 1.0, base=0,
                               channel_multiplier=1).then_inc(s_const, 1)
            pool.iota(node_no[:], [[1, NWX * W]], base=0, channel_multiplier=0,
                      allow_small_or_imprecise_dtypes=True).then_inc(s_const, 1)
            pool.iota(vnum[:], [[1, J]], base=0, channel_multiplier=J,
                      allow_small_or_imprecise_dtypes=True).then_inc(s_const, 1)

            def clear(done):
                pool.memset(acc[:], 0.0).then_inc(s_zero, 1)

            def gather(table, idx, width, l):
                with pool.Fori(0, ITS) as it:
                    for half in range(2):
                        pool.wait_ge(s_free, l * G + it * RING + (half * HALF + 1))
                        pool.tensor_copy(idx_now[:, half, :],
                                         idx[:, bass.ds(it * (RING * J) + half * HALF * J, HALF * J)]).then_inc(s_idx, 1)
                        pool.wait_ge(s_idx, (l * ITS + it) * 2 + half + 1)
                        for k in range(half * HALF, (half + 1) * HALF):
                            stand(pool, s_free, l * G + it * RING + (k + 1))
                            for j in range(J):
                                at = (k - half * HALF) * J + j
                                pool.indirect_dma_start(
                                    ring[:, k, j, 0:width], None, table,
                                    bass.IndirectOffsetOnAxis(idx_now[:, half, at:at + 1], 0)).then_inc(s_row[k], 16)

            pool.wait_ge(s_ready, 1)
            pool.wait_ge(s_vis, 16)
            counts(pool)
            with pool.Fori(0, L) as l:
                stand(pool, s_now, l + 1)
                clear(l)
                stand(pool, s_tab, l * 80 + 80)
                gather(xtab, idx_gat, RW, l)
            pool.wait_ge(s_h, L)
            clear(L)
            pool.wait_ge(s_gt[0], 16 * ((NT + 1) // 2))
            pool.wait_ge(s_gt[1], 16 * (NT // 2))
            gather(gtab, idx_rel, D, L)

        @block.scalar
        def _(act):
            act.dma_start(w_gat[:, :, 0:D], Ws.rearrange("l i o -> i l o")).then_inc(s_w, 16)
            act.dma_start(wd_sb[:], Wd.rearrange("l i o -> i l o")).then_inc(s_w, 16)
            act.dma_start(att_bc[:, 0], att_s.rearrange("l h c -> l (h c)").partition_broadcast(P)).then_inc(s_w, 16)
            act.dma_start(att_bc[:, 1], att_d.rearrange("l h c -> l (h c)").partition_broadcast(P)).then_inc(s_w, 16)
            act.dma_start(bias_gat[:], gat_b.rearrange("l d -> d l"), allow_slow_non_contiguous=True).then_inc(s_w, 16)
            act.dma_start(wr_sb[:], Wr.rearrange("r i o -> i r o")).then_inc(s_w, 16)
            act.dma_start(relb_bc[:], rel_b.rearrange("r o -> (r o)").partition_broadcast(P)).then_inc(s_w, 16)
            act.dma_start(gw_bc[:], gate_w.rearrange("r o k -> (r o k)").partition_broadcast(P)).then_inc(s_w, 16)
            act.dma_start(gateb_bc[:], gate_b.rearrange("r k -> (r k)").partition_broadcast(P)).then_inc(s_w, 16)
            act.dma_start(loop_sb[:], loop_w).then_inc(s_w, 16)
            n_bodies, n_visits, tail = counts(act)
            for s, n in ((s_p, LAG), (s_pc, LAG_SUM)):
                act.sem_inc(s, n)

            def relu(t, b, code):
                act.wait_ge(s_sc, t)
                act.activation(relu4[:, b, :], ps_scores[b][:], ACT.Relu,
                               bias=ad4[:, bass.ds(window_of(act, code), 1)], scale=4.0).then_inc(s_relu, 1)

            def expo(t, k):
                b = k % 2
                act.wait_ge(s_max, t)
                act.activation(pt[:, b, :], nz[:, b, :], ACT.Exp, bias=nmax_new[:, b:b + 1], scale=-1.0)
                act.activation(fade[:, k:k + 1], nmax_old[:, k:k + 1], ACT.Exp, bias=nmax_new[:, b:b + 1],
                               scale=-1.0).then_inc(s_p, 1)

            def weights(t, b):
                act.wait_ge(s_pt, t)
                act.copy(pe_w[:, b].rearrange("p j m -> p (j m)"), ps_w[b][:]).then_inc(s_pc, 1)

            def visits(first, code, back, more):
                for k in range(U):
                    t = act.snap(first + (k + 2))
                    if back or k >= LAG:
                        weights(t, k % 2)
                    if more or k < U - 1:
                        relu(t, 1 - k % 2, code[k])
                    expo(t, k)

            with act.Fori(0, L) as l:
                act.wait_ge(s_now, l + 1)
                for t in range(NT):
                    act.wait_ge(s_t, l * NT + t + 1)
                    act.copy(stage[:, t, 0:D], ps_x[t % 2][:, 0:D])
                    act.activation(stage[:, t, D + 1:RW], ps_x[t % 2][:, D:D + H], ACT.Copy,
                                   scale=SHRINK).then_inc(s_tu, 1)
                stand(act, s_adu, l * NT + NT)
                base = l * n_visits
                code = codes(act, ENG.Activation, 0, U + 1)
                relu(base + 1, 0, code[0])
                visits(base, code[1:], False, True)
                with act.Fori(1, n_bodies - 1) as i:
                    visits(base + i * U, codes(act, ENG.Activation, i * U + 1, U), True, True)
                visits(base + tail, codes(act, ENG.Activation, tail + 1, U - 1), True, False)
                for b in range(LAG):
                    weights(base + n_visits + (b + 2), b)

            act.wait_ge(s_var, 1)
            act.sqrt(rstd[:], rstd[:]).then_inc(s_root, 1)
            for t in range(NT):
                act.wait_ge(s_x1, t + 1)
                act.copy(h_fm[:, t * P:(t + 1) * P], ps_x[t % 2][:, 0:P]).then_inc(s_x1u, 1)
            for t in range(NT):
                b = t % 2
                act.wait_ge(s_gz, t + 1)
                act.activation(ge[:, b, :], gz[:, b, :], ACT.Exp, scale=-1.0).then_inc(s_ge, 1)
                act.wait_ge(s_gate, t + 1)
                if t >= 2:
                    act.wait_ge(s_gt[b], 16 * (t // 2))
                for r in range(NREL):
                    last = act.activation(gmsg[:, b, r * D:(r + 1) * D], msg[:, b, r * D:(r + 1) * D],
                                          ACT.Copy, scale=gate[:, b, r:r + 1])
                last.then_inc(s_gm, 1)
            act.wait_ge(s_var, 2)
            act.sqrt(rstd[:], rstd[:]).then_inc(s_root, 1)

        @block.tensor
        def _(pe):
            pe.wait_ge(s_const, 2)
            n_set = 0

            def bank():
                nonlocal n_set
                if n_set >= 8:
                    pe.wait_ge(s_setf, n_set - 7)
                n_set += 1
                return ps[(n_set - 1) % 8]

            pe.wait_ge(s_rows, 1)
            for k in range(3):
                for r in range(2):
                    o = bank()
                    for j in range(J):
                        last = pe.transpose(o[:, j * GR:(j + 1) * GR], rows_f[k][:, r, j * P:(j + 1) * P],
                                            ident[0:GR, 0:GR])
                    last.then_inc(s_set, 1)
            pe.wait_ge(s_lc, 1)
            o = bank()
            for k in range(4):
                last = pe.matmul(o[:, k * GR:(k + 1) * GR], lhsT=lo_cnt_x[:, k, :], rhs=ident[0:GR, 0:GR],
                                 start=True, stop=True)
            last.then_inc(s_set, 1)
            pe.wait_ge(s_xin, 32)
            for t0 in range(0, NT, 4):
                o = bank()
                for t in range(t0, min(t0 + 4, NT)):
                    last = pe.transpose(o[:, (t - t0) * P:(t - t0 + 1) * P], x_nm[:, t, :], ident[:])
                last.then_inc(s_set, 1)

            n_bodies, n_visits, tail = counts(pe)
            pe.wait_ge(s_vis, 16)
            pe.sem_inc(s_pt, LAG + 1)
            pe.sem_inc(s_sum, LAG_ADD)
            pe.wait_ge(s_ready, 1)

            def scores(t, b):
                pe.wait_ge(s_mask, t)
                for j in range(J):
                    last = pe.transpose(ps_scores[b][:, j * P:(j + 1) * P], lmask[:, b, j, :], ident[:])
                last.then_inc(s_sc, 1)

            def turn(t, b):
                pe.wait_ge(s_p, t)
                for j in range(J):
                    last = pe.transpose(ps_w[b][:, j * P:(j + 1) * P], pt[:, b, j * P:(j + 1) * P], ident[:])
                last.then_inc(s_pt, 1)

            def sums(t, b, slot, weights, s_weights, width):
                pe.wait_ge(s_weights, t)
                for j in range(J):
                    last = pe.matmul(ps_sum[b][:, 0:width], lhsT=weights[:, b, j, :],
                                     rhs=ring_flat[:, bass.ds(slot * (J * RW) + j * RW, width)],
                                     start=(j == 0), stop=(j == J - 1))
                last.then_inc(s_sum, 1)

            def visits(first, code, back):
                for k in range(U):
                    t = pe.snap(first + (k + 1))
                    scores(t, k % 2)
                    if back or k >= LAG_SUM:
                        sums(t, (k - LAG_SUM) % 2, slot_of(pe, code[k - (0 if back else LAG_SUM)]), pe_w, s_pc, AW)
                    if back or k >= LAG:
                        turn(t, k % 2)

            with pe.Fori(0, L) as l:
                pe.wait_ge(s_now, l + 1)
                for t in range(NT):
                    if t >= 2:
                        pe.wait_ge(s_tu, l * NT + t - 1)
                    pe.matmul(ps_x[t % 2][:, 0:D + H], lhsT=h_fm[:, t * P:(t + 1) * P], rhs=w_now[:],
                              start=True, stop=True).then_inc(s_t, 1)
                    if t >= 2:
                        pe.wait_ge(s_adu, l * NT + t - 1)
                    pe.matmul(ps_sum[t % 2][:, 0:P], lhsT=adx_now[:].rearrange("p h w -> p (h w)"),
                              rhs=h_fm[:, t * P:(t + 1) * P], start=True, stop=True).then_inc(s_ad, 1)
                stand(pe, s_adu, l * NT + NT)
                base = l * n_visits
                visits(base, codes(pe, ENG.PE, 0, U - LAG_SUM), False)
                with pe.Fori(1, n_bodies) as i:
                    visits(base + i * U, codes(pe, ENG.PE, i * U - LAG_SUM, U), True)
                code = codes(pe, ENG.PE, tail + (U - LAG_SUM), LAG_SUM)
                for k in range(LAG_SUM):
                    t = pe.snap(base + n_visits + (k + 1))
                    stand(pe, s_added, l * LAG_SUM + (k + 1))
                    sums(t, (k - LAG_SUM) % 2, slot_of(pe, code[k]), pe_w, s_pc, AW)
                    if k < LAG:
                        turn(t, k)

            pe.wait_ge(s_h, L)
            for t in range(NT):
                if t >= 2:
                    pe.wait_ge(s_nu, t - 1)
                pe.transpose(ps_sum[t % 2][:, 0:P], h_fm[:, t * P:(t + 1) * P], ident[:]).then_inc(s_n, 1)
            for t in range(NT):
                pe.wait_ge(s_norm, t + 1)
                if t >= 2:
                    pe.wait_ge(s_x1u, t - 1)
                pe.transpose(ps_x[t % 2][:, 0:P], x_nm[:, t, :], ident[:]).then_inc(s_x1, 1)
            for t in range(NT):
                b = t % 2
                pe.wait_ge(s_x1u, t + 1)
                if t >= 2:
                    pe.wait_ge(s_mu, t - 1)
                tile = h_fm[:, t * P:(t + 1) * P]
                for q in range(2):
                    pe.matmul(ps[2 * b + q][:], lhsT=tile,
                              rhs=wr_sb[:, q * NREL // 2:(q + 1) * NREL // 2, :].rearrange("p r o -> p (r o)"),
                              start=True, stop=True)
                pe.matmul(ps_sum[b][:, 0:NREL], lhsT=tile, rhs=wg[:], start=True, stop=True).then_inc(s_m, 1)
            base = n_visits * L
            pe.wait_ge(s_mu, NT)
            with pe.Fori(0, n_bodies) as i:
                code = codes(pe, ENG.PE, i * U, U)
                for k in range(U):
                    sums(pe.snap(base + i * U + (k + 1)), k % 2, slot_of(pe, code[k]), lmask, s_mask, D)
            pe.wait_ge(s_h, L + 1)
            for t in range(NT):
                if t >= 2:
                    pe.wait_ge(s_nu, NT + t - 1)
                pe.matmul(ps_sum[t % 2][:, 0:D], lhsT=h_fm[:, t * P:(t + 1) * P], rhs=loop_sb[:],
                          start=True, stop=False)
                pe.matmul(ps_sum[t % 2][:, 0:D], lhsT=diag_t[:, t * P:(t + 1) * P], rhs=ident[:],
                          start=False, stop=True).then_inc(s_n, 1)

        @block.vector
        def _(dve):
            dve.sem_inc(s_max, 1)
            dve.memset(rows_i[0][:, 1, :], PAD_DST)
            dve.memset(rows_i[1][:, 1, :], 0)
            dve.memset(rows_i[2][:, 1, :], 0)
            dve.memset(x_nm[:, NT - 1, :], 0.0).then_inc(s_pad, 1)
            dve.wait_ge(s_edge, 16 * 9)
            for k in range(3):
                dve.tensor_copy(rows_f[k][:], rows_i[k][:])
            dve.drain()
            dve.scalar_tensor_tensor(rows_f[2][:], rows_f[1][:], float(NREL), rows_f[2][:], ALU.mult,
                                     ALU.add).then_inc(s_rows, 1)
            dve.tensor_reduce(mm[:, 0:2], rows_f[0][:], AX, ALU.min)
            dve.tensor_reduce(mm[:, 2:4], rows_f[0][:], AX, ALU.max)
            dve.drain()
            dve.tensor_copy(mmi[:], mm[:])
            dve.drain()
            dve.tensor_single_scalar(mmi[:], mmi[:], 5, ALU.arith_shift_right)
            dve.drain()
            dve.tensor_copy(lo_cnt[:], mmi[:])
            dve.drain()
            dve.scalar_tensor_tensor(lo_cnt[:, 2:4], lo_cnt[:, 2:4], 1.0, lo_cnt[:, 0:2], ALU.add, ALU.subtract)
            dve.drain()
            dve.tensor_copy(lo_cnt_x[:], lo_cnt[:].unsqueeze(2).to_broadcast([GR, 4, P])).then_inc(s_lc, 1)

            n_set = 0
            for target in (dst_e[:], idx_gat[:].rearrange("p (g j) -> p g j", j=J),
                           idx_rel[:].rearrange("p (g j) -> p g j", j=J)):
                for r in range(2):
                    dve.wait_ge(s_set, n_set + 1)
                    dve.tensor_copy(target[:, r * GR:(r + 1) * GR, :].rearrange("p g j -> p j g"),
                                    ps[n_set % 8][:, 0:J * GR].rearrange("p (j g) -> p j g", j=J)).then_inc(s_setf, 1)
                    n_set += 1
            dve.memset(ones_g, 1.0)
            dve.memset(step_k, 128.0 + 32768.0)
            dve.drain()
            dve.memset(step_k.rearrange("p (i k) -> p i k", k=RING)[:, :, 0:1], 128.0 - 32768.0 * (RING - 1))
            dve.drain()
            dve.memset(step_k[:, 0:1], 0.0)
            dve.wait_ge(s_set, n_set + 1)
            low, cnt = (ps[n_set % 8][:, k * G:(k + 1) * G] for k in range(2))
            dve.tensor_tensor_scan(incl, ones_g, cnt, 0.0, ALU.mult, ALU.add)
            dve.drain()
            dve.tensor_tensor(off, incl, cnt, ALU.subtract)
            dve.drain()
            dve.tensor_tensor(gap, low, off, ALU.subtract).then_inc(s_setf, 1)
            n_set += 1
            dve.drain()
            dve.tensor_tensor(step_k[:, 1:G], step_k[:, 1:G], gap[:, 1:G], ALU.add)
            dve.tensor_copy(lead[:, 0:1], gap[:, 0:1])
            dve.drain()
            dve.tensor_tensor(step_k[:, 1:G], step_k[:, 1:G], gap[:, 0:G - 1], ALU.subtract)
            dve.tensor_tensor(step_k[:, 0:1], step_k[:, 0:1], lead[:, 0:1], ALU.add)
            dve.tensor_copy(incl_i[:], incl[0:1, :])
            dve.tensor_scalar(ctl_f[:], incl[0:1, G - 1:G], float(U - 1), None, ALU.add)
            dve.drain()
            dve.tensor_copy(ctl[:, 0:1], ctl_f[:])
            dve.drain()
            dve.tensor_single_scalar(ctl[:, 0:1], ctl[:, 0:1], U.bit_length() - 1, ALU.arith_shift_right)
            dve.drain()
            dve.tensor_single_scalar(ctl[:, 1:2], ctl[:, 0:1], U, ALU.mult)
            dve.drain()
            dve.tensor_single_scalar(ctl[:, 2:3], ctl[:, 1:2], VB, ALU.add)
            dve.tensor_copy(incl_i[:, G - 1:G], ctl[:, 1:2])
            dve.drain()
            dve.tensor_single_scalar(ctl[:, 2:3], ctl[:, 2:3], VB.bit_length() - 1, ALU.arith_shift_right)
            dve.drain()
            dve.tensor_single_scalar(ctl[:, 3:4], ctl[:, 1:2], -U, ALU.add).then_inc(s_ctl, 1)
            n_bodies, n_visits, tail = counts(dve)
            n_blocks = dve.value_load(ctl[0:1, 2:3], min_val=1, max_val=VMAX // VB)

            for t0 in range(0, NT, 4):
                m = min(4, NT - t0) * P
                dve.wait_ge(s_set, n_set + 1)
                dve.tensor_copy(h_fm[:, t0 * P:t0 * P + m], ps[n_set % 8][:, 0:m]).then_inc(s_setf, 1)
                n_set += 1
            dve.wait_ge(s_w, 16 * 10)
            fold_l = fold[:, 0:D]
            for l in range(L):
                for k, w, o in ((0, w_gat[:, l, 0:D], w_gat[:, l, D:D + H]), (1, wd_sb[:, l, :], ad_w[:, l, :])):
                    dve.tensor_tensor(fold_l, w, att_bc[:, k, l, :], ALU.mult)
                    dve.drain()
                    dve.tensor_reduce(o, fold_l.rearrange("p (h c) -> p h c", h=H), AX, ALU.add)
                    dve.drain()
            dve.tensor_tensor(fold, wr_sb[:].rearrange("p r o -> p (r o)"), gw_bc[:], ALU.mult)
            dve.drain()
            dve.tensor_reduce(wg[:], fold.rearrange("p (r o) -> p r o", r=NREL), AX, ALU.add)
            dve.drain()
            dve.tensor_tensor(fold, relb_bc[:], gw_bc[:], ALU.mult)
            dve.drain()
            dve.tensor_reduce(gbias[:], fold.rearrange("p (r o) -> p r o", r=NREL), AX, ALU.add)
            dve.drain()
            dve.tensor_tensor(gbias[:], gbias[:], gateb_bc[:], ALU.add)
            dve.memset(relu_floor[:, 0:L - 1], 0.0)
            dve.memset(relu_floor[:, L - 1:L], -3.0e38)
            dve.memset(stage[:, :, D:D + 1], 1.0)
            dve.wait_ge(s_const, 4)
            dve.tensor_reduce(eye_w[:], ident[:].rearrange("p (h n) -> p n h", h=H), AX, ALU.add)
            dve.drain()
            dve.nop().then_inc(s_ready, 1)

            with dve.Fori(0, n_blocks) as b:
                dve.tensor_tensor(vge, vnum[:].unsqueeze(2).to_broadcast([P, J, G]),
                                  off.unsqueeze(1).to_broadcast([P, J, G]), ALU.is_ge)
                dve.drain()
                dve.tensor_tensor(vwt, vge, step_k.unsqueeze(1).to_broadcast([P, J, G]), ALU.mult)
                dve.drain()
                dve.tensor_reduce(vsum, vwt, AX, ALU.add)
                dve.drain()
                dve.tensor_tensor(vcode[:], vsum, vnum[:], ALU.add).then_inc(s_code, 1)
                dve.drain()
                dve.tensor_scalar(vnum[:], vnum[:], float(VB), None, ALU.add)
                stand(dve, s_vis, b * 16 + 16)
                dve.drain()

            def rows_landed(group, l):
                dve.wait_ge(s_landed, group + (l * G + 1))

            def members(group, window, n_rep):
                d = dst_e[:].rearrange("p g j -> p (g j)")[:, bass.ds(group * J, J)]
                n = node_no[:, bass.ds(window * W, W)]
                if n_rep == 1:
                    return (d.unsqueeze(2).to_broadcast([P, J, W]), n.unsqueeze(1).to_broadcast([P, J, W]))
                return (d.unsqueeze(2).unsqueeze(3).to_broadcast([P, J, H, W]),
                        n.unsqueeze(1).unsqueeze(2).to_broadcast([P, J, H, W]))

            def mask_dist(b, code, l):
                group = group_of(dve, code)
                rows_landed(group, l)
                d, n = members(group, window_of(dve, code), 1)
                dve.tensor_tensor(dist[:, b], d, n, ALU.not_equal)

            def mask_scores(b, code):
                slot = slot_of(dve, code) * (J * RW)
                rows = ring_flat[:, bass.ds(slot, J * RW)].rearrange("p (j c) -> p j c", c=RW)[:, :, D + 1:RW]
                dve.tensor_tensor(lmask[:, b].rearrange("p j (h n) -> p j h n", h=H),
                                  rows.unsqueeze(3).to_broadcast([P, J, H, W]),
                                  dist[:, b].unsqueeze(2).to_broadcast([P, J, H, W]),
                                  ALU.subtract).then_inc(s_mask, 1)

            def add(t, k, code):
                b = (k - LAG_ADD) % 2
                dve.wait_ge(s_sum, t)
                s = acc[:, bass.ds(window_of(dve, code) * AW, AW)]
                return dve.scalar_tensor_tensor(s, s, fade[:, k:k + 1], ps_sum[b][:, 0:AW], ALU.mult, ALU.add)

            def keep_max(b, code):
                dve.tensor_copy(nmax[:, bass.ds(window_of(dve, code), 1)], nmax_new[:, b:b + 1])

            def step(t, k, old, last, code, ahead, l):
                b = k % 2
                if old is not None:
                    added = add(t, (k - LAG_ADD) % U, old)
                    if ahead is None:
                        added.then_inc(s_added, 1)
                if ahead is not None:
                    mask_dist(1 - b, ahead, l)
                if last is not None:
                    dve.drain()
                    keep_max(1 - b, last)
                dve.drain()
                dve.tensor_copy(nmax_old[:, k:k + 1], nmax[:, bass.ds(window_of(dve, code), 1)])
                dve.drain()
                if ahead is not None:
                    mask_scores(1 - b, ahead)
                stand(dve, s_relu, t)
                dve.tensor_tensor_reduce(nz[:, b, :], ps_scores[b][:], relu4[:, b, :], -SLOPE / SHRINK,
                                         nmax_old[:, k:k + 1], ALU.add, ALU.min,
                                         nmax_new[:, b:b + 1]).then_inc(s_max, 1)

            def visits(first, code, l, back, more):
                for k in range(U):
                    t = dve.snap(first + (k + 1))
                    step(t, k, code[k] if back or k >= LAG_ADD else None,
                         code[LAG_ADD + k - 1] if back or k >= 1 else None, code[LAG_ADD + k],
                         code[LAG_ADD + k + 1] if more or k < U - 1 else None, l)

            def to_feature_major(scaled):
                for h in range(H):
                    rows = slice(h * W, (h + 1) * W)
                    o = diag[rows, :].rearrange("p (w c) -> p w c", c=C)
                    s = acc_w[rows, :, h * C:(h + 1) * C]
                    if scaled:
                        dve.tensor_tensor(o, s, rden[rows, :].unsqueeze(2).to_broadcast([W, NW, C]), ALU.mult)
                    else:
                        dve.tensor_copy(o, s)
                dve.drain()
                dve.transpose(diag_t, diag)
                dve.drain()

            with dve.Fori(0, L) as l:
                dve.tensor_copy(w_now[:], w_gat[:, bass.ds(l, 1), :].rearrange("p l o -> p (l o)"))
                dve.tensor_copy(adx_now[:], ad_w[:, bass.ds(l, 1), :].rearrange("p l h -> p (l h)")
                                .unsqueeze(2).to_broadcast([P, H, W])).then_inc(s_now, 1)
                for t in range(NT):
                    dve.wait_ge(s_ad, l * NT + t + 1)
                    picked = relu4[:, 0, 0:P].rearrange("p (w n) -> p w n", n=W)
                    dve.scalar_tensor_tensor(picked, ps_sum[t % 2][:, 0:P].rearrange("p (w n) -> p w n", n=W), 4.0 * SHRINK,
                                             eye_w[:].unsqueeze(1).to_broadcast([P, H, W]), ALU.mult,
                                             ALU.mult).then_inc(s_adu, 1)
                    dve.drain()
                    dve.tensor_reduce(ad4[:, t * H:(t + 1) * H], picked, AX, ALU.add)
                    dve.drain()
                dve.memset(nmax[:], FLOOR)
                dve.memset(ad4[:, NW:NWX], 0.0)
                stand(dve, s_zero, l + 1)
                base = l * n_visits
                code = codes(dve, ENG.DVE, 0, U + 1)
                mask_dist(0, code[0], l)
                dve.drain()
                mask_scores(0, code[0])
                visits(base, (None,) * LAG_ADD + tuple(code), l, False, True)
                with dve.Fori(1, n_bodies - 1) as i:
                    visits(base + i * U, codes(dve, ENG.DVE, i * U - LAG_ADD, U + LAG_ADD + 1), l, True, True)
                code = codes(dve, ENG.DVE, tail - LAG_ADD, U + LAG_ADD)
                visits(base + tail, code, l, True, False)
                for k in range(LAG_ADD):
                    dve.drain()
                    added = add(base + n_visits + (k + 1), (k - LAG_ADD) % U, code[U + k])
                    if k < LAG_ADD - LAG:
                        added.then_inc(s_added, 1)
                dve.drain()
                dve.tensor_scalar(rden[:], acc_w[:, :, D:D + 1].rearrange("p w c -> p (w c)"), EPS_DEN, None, ALU.add)
                dve.drain()
                dve.reciprocal(rden[:], rden[:])
                dve.drain()
                to_feature_major(True)
                dve.tensor_scalar(h_fm[:], diag_t, bias_gat[:, bass.ds(l, 1)], relu_floor[:, bass.ds(l, 1)],
                                  ALU.add, ALU.max).then_inc(s_h, 1)
                dve.drain()

            def norm(first, relu_first):
                for t in range(NT):
                    dve.wait_ge(s_n, first + t + 1)
                    if relu_first:
                        dve.scalar_tensor_tensor(x_nm[:, t, :], ps_sum[t % 2][:, 0:D], 0.0, x_nm[:, t, :],
                                                 ALU.max, ALU.add).then_inc(s_nu, 1)
                    else:
                        dve.tensor_tensor(x_nm[:, t, :], ps_sum[t % 2][:, 0:D], x_nm[:, t, :],
                                          ALU.add).then_inc(s_nu, 1)
                    dve.drain()
                    dve.bn_stats(bn6[:, t, :], x_nm[:, t, :])
                    dve.drain()
                    dve.bn_aggr(mv[:, t, :], bn6[:, t, :])
                dve.drain()
                dve.tensor_scalar(rstd[:], mv[:, :, 1], EPS_LN, None, ALU.add).then_inc(s_var, 1)
                dve.wait_ge(s_root, 2 if relu_first else 1)
                dve.reciprocal(rstd[:], rstd[:])
                dve.drain()
                for t in range(NT):
                    dve.tensor_scalar(x_nm[:, t, :], x_nm[:, t, :], mv[:, t, 0:1], rstd[:, t:t + 1],
                                      ALU.subtract, ALU.mult).then_inc(s_norm, 1)

            norm(0, False)
            for t in range(NT):
                b = t % 2
                dve.wait_ge(s_m, t + 1)
                if t >= 2:
                    dve.wait_ge(s_gm, t - 1)
                dve.tensor_tensor(gz[:, b, :], ps_sum[b][:, 0:NREL], gbias[:], ALU.add).then_inc(s_gz, 1)
                for q in range(2):
                    last = dve.tensor_tensor(msg[:, b, q * 512:(q + 1) * 512], ps[2 * b + q][:],
                                             relb_bc[:, q * 512:(q + 1) * 512], ALU.add)
                last.then_inc(s_mu, 1)
                dve.wait_ge(s_ge, t + 1)
                dve.tensor_scalar(gate[:, b, :], ge[:, b, :], 1.0, None, ALU.add)
                dve.drain()
                dve.reciprocal(gate[:, b, :], gate[:, b, :]).then_inc(s_gate, 1)

            dve.wait_ge(s_zero, L + 1)
            base = n_visits * L

            def match(b, code):
                group = group_of(dve, code)
                rows_landed(group, L)
                d, n = members(group, window_of(dve, code), H)
                dve.tensor_tensor(lmask[:, b].rearrange("p j (h n) -> p j h n", h=H), d, n,
                                  ALU.is_equal).then_inc(s_mask, 1)

            def add_plain(t, b, code):
                dve.wait_ge(s_sum, t)
                s = acc[:, bass.ds(window_of(dve, code) * AW, D)]
                dve.tensor_tensor(s, s, ps_sum[b][:, 0:D], ALU.add)

            code = codes(dve, ENG.DVE, 0, U)
            for k in range(U):
                if k >= LAG:
                    add_plain(base + (k + 1 - LAG + LAG_ADD), k % 2, code[k - LAG])
                match(k % 2, code[k])
                dve.drain()
            with dve.Fori(1, n_bodies) as i:
                code = codes(dve, ENG.DVE, i * U - LAG, U + LAG)
                for k in range(U):
                    add_plain(base + i * U + (k + 1 - LAG + LAG_ADD), k % 2, code[k])
                    match(k % 2, code[k + LAG])
                    dve.drain()
            code = codes(dve, ENG.DVE, tail + (U - LAG), LAG)
            for b in range(LAG):
                add_plain(base + n_visits + (b + 1 - LAG + LAG_ADD), b, code[b])
                dve.drain()
            to_feature_major(False)
            dve.nop().then_inc(s_h, 1)
            norm(NT, True)


_INS = ["x", "src", "dst", "edge_type_8", "L0_gnn_Ws", "L0_gnn_Wd", "L0_gnn_att_s", "L0_gnn_att_d", "L0_gnn_b",
        "L1_gnn_W", "L1_gnn_bias_term", "L1_gnn_gate_weight", "L1_gnn_gate_bias", "L1_gnn_loop_weight"]


def kernel(**inputs):
    import numpy as _np
    import concourse.bacc as _bacc
    from concourse import mybir as _mybir
    from concourse.bass_utils import run_bass_kernel_spmd as _run

    nc = _bacc.Bacc("TRN2", target_bir_lowering=False, num_devices=1)
    arrays, args = {}, []
    for name in _INS:
        a = _np.ascontiguousarray(inputs[name])
        arrays[f"in_{name}_dram"] = a
        args.append(nc.dram_tensor(f"in_{name}_dram", a.shape, _mybir.dt.from_np(a.dtype), kind="ExternalInput").ap())
    result = nc.dram_tensor("out_0_dram", (N, D), F32, kind="ExternalOutput").ap()
    build(nc, *args, result)
    r = _run(nc, [arrays], core_ids=[0])
    return r.results[0]["out_0_dram"]
```

```python
from contextlib import ExitStack

import concourse.bass as bass
from concourse import mybir

F32 = mybir.dt.float32
I32 = mybir.dt.int32
ALU = mybir.AluOpType
ACT = mybir.ActivationFunctionType
AX = mybir.AxisListType.X
ENG = mybir.EngineType

P = 128
N = 3125
E = 100000
D = 128
H = 4
C = D // H
L = 3
NREL = 8
SLOPE = 0.2
EPS_DEN = 1e-16
EPS_LN = 1e-5

W = P // H
J = 4
GE = J * P
GR = 98
G = 2 * GR
NT = (N + P - 1) // P
NP = NT * P
U = 8
PARTS = 5
TP = NT // PARTS
GBUF = 4
R_DVE = 3
T0 = 3
LAG = 2
LAG_SUM = 3
LAG_ADD = 4
NW = NP // W
PAD_DST = (N + W - 1) // W * W - 1
NWX = PAD_DST // W + U
RING = 14
ITS = G // RING
HALF = RING // 2
LAG_FREE = 10
RW = D + 1 + H
AW = D + 1
SHRINK = 2.0 ** -64
FLOOR = 1e15
VB = 512
VMAX = G * (N // W + 1) + 2 * VB
assert RING * ITS == G and PARTS * TP == NT and T0 * RW <= 512 and PAD_DST < NP and NWX >= NW


def build(nc, x, src, dst, et, Ws, Wd, att_s, att_d, gat_b, Wr, rel_b, gate_w, gate_b, loop_w, out):
    with ExitStack() as ctx:
        def sb(name, shape, dt=F32):
            return ctx.enter_context(nc.sbuf_tensor(name, shape, dt))

        def sem(name):
            return ctx.enter_context(nc.semaphore(name))

        xtab = nc.dram_tensor("xtab", (NP, RW), F32).ap()
        gtab = nc.dram_tensor("gtab", (NP * NREL, D), F32).ap()
        vis = nc.dram_tensor("vis", (VMAX,), I32).ap()

        ident = sb("ident", [P, P])
        eye_w = sb("eye_w", [P, W])
        node_no = sb("node_no", [P, NWX * W])
        x_nm = sb("x_nm", [P, NT, D])
        h_fm = sb("h_fm", [P, NP])
        acc = sb("acc", [P, NWX * AW])
        ring = sb("ring", [P, RING, J, RW])
        stage = sb("stage", [P, NT, RW])
        dst_e = sb("dst_e", [P, G, J])
        idx_gat = sb("idx_gat", [P, G * J], I32)
        idx_rel = sb("idx_rel", [P, G * J], I32)
        idx_now = sb("idx_now", [P, 2, HALF * J], I32)
        w_gat = sb("w_gat", [P, L, D + H])
        wd_sb = sb("wd_sb", [P, L, D])
        ad_w = sb("ad_w", [P, L + 1, H])
        adx_now = sb("adx_now", [P, H, W])
        bias_gat = sb("bias_gat", [P, L])
        relu_floor = sb("relu_floor", [P, L])
        att_bc = sb("att_bc", [P, 2, L, D])
        ad4 = sb("ad4", [P, NWX])
        nmax = sb("nmax", [P, NWX])
        rden = sb("rden", [P, NW])
        dist = sb("dist", [P, 2, J, W])
        lmask = sb("lmask", [P, 2, J, P])
        relu4 = sb("relu4", [P, 2, GE])
        nz = sb("nz", [P, 2, GE])
        nmax_old = sb("nmax_old", [P, U])
        nmax_new = sb("nmax_new", [P, 2])
        pt = sb("pt", [P, 2, GE])
        fade = sb("fade", [P, U])
        pe_w = sb("pe_w", [P, 2, J, P])
        wr_sb = sb("wr_sb", [P, NREL, D])
        relb_bc = sb("relb_bc", [P, NREL * D])
        gw_bc = sb("gw_bc", [P, NREL * D])
        gateb_bc = sb("gateb_bc", [P, NREL])
        wg = sb("wg", [P, NREL])
        gbias = sb("gbias", [P, NREL])
        gz = sb("gz", [P, NT, NREL])
        ge = sb("ge", [P, NT, NREL])
        gate = sb("gate", [P, NT, NREL])
        loop_sb = sb("loop_sb", [P, D])
        bn6 = sb("bn6", [P, NT, 6])
        mv = sb("mv", [P, NT, 2])
        rstd = sb("rstd", [P, NT])
        vcode = sb("vcode", [P, J], I32)
        vnum = sb("vnum", [P, J])
        ctl_f = sb("ctl_f", [1, 1])
        ctl = sb("ctl", [1, 4], I32)
        incl_i = sb("incl_i", [1, G], I32)

        acc_w = acc[:].rearrange("p (w c) -> p w c", c=AW)
        ring_flat = ring[:].rearrange("p r j c -> p (r j c)")
        acc_w = acc_w[:, 0:NW, :]
        diag = ring_flat[:, 0:NP]
        diag_t = ring_flat[:, NP:2 * NP]
        msg = ring_flat[:, 0:2 * NREL * D].rearrange("p (b m) -> p b m", b=2)
        gmsg = ring_flat[:, 2 * NREL * D:(2 + GBUF) * NREL * D].rearrange("p (b m) -> p b m", b=GBUF)
        ring_i, ring_f = (ring_flat[0:GR, k * 3072:(k + 1) * 3072].rearrange("p (k r e) -> p k r e", k=3, r=2)
                          for k in range(2))
        rows_i = [ring_i[:, k].bitcast(I32) for k in range(3)]
        rows_f = [ring_f[:, k] for k in range(3)]
        mm = ring_flat[0:GR, 6144:6148]
        mmi = ring_flat[0:GR, 6148:6152].bitcast(I32)
        lo_cnt = ring_flat[0:GR, 6152:6156]
        lo_cnt_x = ring_flat[0:GR, 6156:6156 + 4 * P].rearrange("p (k m) -> p k m", k=4)
        vrow = ring_flat[:, 0:6 * G].rearrange("p (k g) -> p k g", k=6)
        ones_g, incl, off, gap, step_k, lead = (vrow[:, k, :] for k in range(6))
        vsum = ring_flat[:, 6 * G:6 * G + J]
        vge = nz[:].rearrange("p b e -> p (b e)")[:, 0:J * G].rearrange("p (q g) -> p q g", q=J)
        vwt = pt[:].rearrange("p b e -> p (b e)")[:, 0:J * G].rearrange("p (q g) -> p q g", q=J)
        fold = pe_w[:].rearrange("p b j m -> p (b j m)")

        ps = [ctx.enter_context(nc.psum_tensor(f"bank{i}", [P, 512], F32)) for i in range(8)]
        ps_scores, ps_w, ps_sum, ps_x = ps[0:2], ps[2:4], ps[4:6], ps[6:8]
        ps_table, ps_target, ps_gate = ps[0:4], ps[4:8], ps[7]

        s_const = sem("s_const")
        s_wg = sem("s_wg")
        s_w = sem("s_w")
        s_xin = sem("s_xin")
        s_edge = sem("s_edge")
        s_pad = sem("s_pad")
        s_rows = sem("s_rows")
        s_set = sem("s_set")
        s_setf = sem("s_setf")
        s_lc = sem("s_lc")
        s_ctl = sem("s_ctl")
        s_code = sem("s_code")
        s_vis = sem("s_vis")
        s_ready = sem("s_ready")
        s_folded = sem("s_folded")
        s_read = sem("s_read")
        s_h = sem("s_h")
        s_t = sem("s_t")
        s_tu = sem("s_tu")
        s_ad = sem("s_ad")
        s_adu = sem("s_adu")
        s_tab = sem("s_tab")
        s_zero = sem("s_zero")
        s_idx = sem("s_idx")
        s_row = [sem(f"s_row{k}") for k in range(RING)]
        s_landed = sem("s_landed")
        s_free = sem("s_free")
        s_p = sem("s_p")
        s_pt = sem("s_pt")
        s_pc = sem("s_pc")
        s_sum = sem("s_sum")
        s_added = sem("s_added")
        s_mask = sem("s_mask")
        s_sc = sem("s_sc")
        s_relu = sem("s_relu")
        s_max = sem("s_max")
        s_n = sem("s_n")
        s_nu = sem("s_nu")
        s_var = sem("s_var")
        s_root = sem("s_root")
        s_norm = sem("s_norm")
        s_x1 = sem("s_x1")
        s_x1u = sem("s_x1u")
        s_g = sem("s_g")
        s_m = sem("s_m")
        s_mu = sem("s_mu")
        s_gz = sem("s_gz")
        s_ge = sem("s_ge")
        s_gate = sem("s_gate")
        s_gm = sem("s_gm")
        s_gd = sem("s_gd")
        s_gt = [sem(f"s_gt{b}") for b in range(GBUF)]
        s_stood = sem("s_stood")
        s_out = sem("s_out")

        block = ctx.enter_context(nc.Block())
        edge_lists = (dst, src, et)
        full_rows = E // GE - GR
        tail = E - (GR + full_rows) * GE

        def stand(eng, s, value):
            eng.wait_ge(s, value)
            eng.sem_inc(s_stood, 1)

        def counts(eng):
            eng.wait_ge(s_ctl, 1)
            n_bodies = eng.value_load(ctl[0:1, 0:1], min_val=G // U, max_val=VMAX // U)
            n_visits = eng.value_load(ctl[0:1, 1:2], min_val=G, max_val=VMAX)
            tail = eng.value_load(ctl[0:1, 3:4], min_val=G - U, max_val=VMAX - 2 * U)
            return n_bodies, n_visits, tail

        def codes(eng, kind, first, n):
            _, got = nc.values_load_multi_w_load_instructions(
                vis[bass.ds(first, n)].rearrange("(a b) -> a b", a=1), engines=[kind], min_val=0,
                max_val=(RING << 15) - 1, skip_runtime_bounds_check_because="made on chip from slot, group and window")
            return got

        def table_tiles():
            return [(ps_table[(2 * m + k) % 4], m * TP + k * T0, (T0, TP - T0)[k]) for m in range(PARTS) for k in range(2)]

        MADE = "the codes are made on chip from slot, group and window numbers"

        def slot_of(eng, code):
            return nc.s_assert_within(code >> 15, 0, RING - 1, skip_runtime_bounds_check_because=MADE)

        def group_of(eng, code):
            return nc.s_assert_within((code >> 7) & 255, 0, G - 1, skip_runtime_bounds_check_because=MADE)

        def window_of(eng, code):
            return nc.s_assert_within(code & 127, 0, NWX - 1, skip_runtime_bounds_check_because=MADE)

        @block.sync
        def _(sp):
            for k, a in enumerate(edge_lists):
                sp.dma_start(rows_i[k][:, 0, :], a[0:GR * GE].rearrange("(p e) -> p e", e=GE)).then_inc(s_edge, 16)
            sp.wait_ge(s_pad, 1)
            nf = N // P
            sp.dma_start(x_nm[:, 0:nf, :], x[0:nf * P, :].rearrange("(t p) d -> p t d", p=P)).then_inc(s_xin, 16)
            sp.dma_start(x_nm[0:N - nf * P, nf, :], x[nf * P:N, :]).then_inc(s_xin, 16)
            for k, a in enumerate(edge_lists):
                sp.dma_start(rows_i[k][0:full_rows, 1, :],
                             a[GR * GE:(GR + full_rows) * GE].rearrange("(p e) -> p e", e=GE)).then_inc(s_edge, 16)
                sp.dma_start(rows_i[k][full_rows:GR, 1, 0:tail],
                             a[(GR + full_rows) * GE:E].rearrange("(p e) -> p e", p=1)).then_inc(s_edge, 16)
            sp.wait_ge(s_ctl, 1)
            n_blocks = sp.value_load(ctl[0:1, 2:3], min_val=1, max_val=VMAX // VB)
            _, n_visits, _ = counts(sp)
            with sp.Fori(0, n_blocks) as b:
                sp.wait_ge(s_code, b + 1)
                sp.dma_start(vis[bass.ds(b * VB, VB)].rearrange("(p q) -> p q", q=J), vcode[:]).then_inc(s_vis, 16)

            sp.sem_inc(s_free, RING)

            def follow(base, landed0, its0):
                def landed(it, k):
                    sp.wait_ge(s_row[k], (it + its0 + 1) * (16 * J))
                    sp.sem_inc(s_landed, 1)

                def free(g):
                    last = sp.value_load(incl_i[0:1, bass.ds(g, 1)], min_val=1, max_val=VMAX)
                    sp.wait_ge(s_sum, base + last + LAG_ADD)
                    sp.sem_inc(s_free, 1)

                for k in range(RING):
                    landed(0, k)
                    if k >= LAG_FREE:
                        free(k - LAG_FREE)
                with sp.Fori(1, ITS) as it:
                    for k in range(RING):
                        landed(it, k)
                        free(it * RING + (k - LAG_FREE))
                for g in range(G - LAG_FREE, G):
                    free(g)

            with sp.Fori(0, L) as l:
                for m in range(PARTS):
                    sp.wait_ge(s_tu, (l * PARTS + m + 1) * 2)
                    sp.dma_start(xtab[m * TP * P:(m + 1) * TP * P, :].rearrange("(t p) c -> p t c", p=P),
                                 stage[:, m * TP:(m + 1) * TP, :]).then_inc(s_tab, 16)
                follow(l * n_visits, l * G, l * ITS)
            for t in range(NT):
                sp.wait_ge(s_gm, t + 1)
                sp.wait_ge(s_gd, t + 1)
                sp.dma_start(gtab[t * P * NREL:(t + 1) * P * NREL, :].rearrange("(p r) d -> p (r d)", r=NREL),
                             gmsg[:, t % GBUF, :]).then_inc(s_gt[t % GBUF], 16)
            follow(n_visits * L, L * G, L * ITS)
            for t0 in range(0, nf, 6):
                t1 = min(t0 + 6, nf)
                sp.wait_ge(s_norm, NT + t1)
                sp.dma_start(out[t0 * P:t1 * P, :].rearrange("(t p) d -> p t d", p=P), x_nm[:, t0:t1, :]).then_inc(s_out, 16)
            sp.wait_ge(s_norm, 2 * NT)
            sp.dma_start(out[nf * P:N, :], x_nm[0:N - nf * P, nf, :]).then_inc(s_out, 16)
            sp.wait_ge(s_out, 16 * ((nf + 5) // 6 + 1))

        @block.gpsimd
        def _(pool):
            pool.memset(ident[:], 0.0).then_inc(s_const, 1)
            pool.wait_ge(s_const, 1)
            pool.affine_select(ident[:], ident[:], [[-1, P]], ALU.not_equal, 1.0, base=0,
                               channel_multiplier=1).then_inc(s_const, 1)
            pool.iota(node_no[:], [[1, NWX * W]], base=0, channel_multiplier=0,
                      allow_small_or_imprecise_dtypes=True).then_inc(s_const, 1)
            pool.iota(vnum[:], [[1, J]], base=0, channel_multiplier=J,
                      allow_small_or_imprecise_dtypes=True).then_inc(s_const, 1)

            def clear(l):
                for m in range(PARTS):
                    if isinstance(l, int):
                        pool.wait_ge(s_read, l * PARTS + m + 1)
                    else:
                        stand(pool, s_read, l * PARTS + m + 1)
                    end = NWX if m == PARTS - 1 else (m + 1) * TP * H
                    pool.memset(acc[:, m * TP * H * AW:end * AW], 0.0).then_inc(s_zero, 1)

            def gather(table, idx, width, l):
                with pool.Fori(0, ITS) as it:
                    for half in range(2):
                        pool.wait_ge(s_free, l * G + it * RING + (half * HALF + 1))
                        pool.tensor_copy(idx_now[:, half, :],
                                         idx[:, bass.ds(it * (RING * J) + half * HALF * J, HALF * J)]).then_inc(s_idx, 1)
                        pool.wait_ge(s_idx, (l * ITS + it) * 2 + half + 1)
                        for k in range(half * HALF, (half + 1) * HALF):
                            stand(pool, s_free, l * G + it * RING + (k + 1))
                            for j in range(J):
                                at = (k - half * HALF) * J + j
                                pool.indirect_dma_start(
                                    ring[:, k, j, 0:width], None, table,
                                    bass.IndirectOffsetOnAxis(idx_now[:, half, at:at + 1], 0)).then_inc(s_row[k], 16)

            counts(pool)
            with pool.Fori(0, L) as l:
                clear(l)
                pool.wait_ge(s_ready, 1)
                stand(pool, s_tab, (l + 1) * (16 * PARTS))
                gather(xtab, idx_gat, RW, l)
            clear(L)
            for b in range(GBUF):
                pool.wait_ge(s_gt[b], 16 * ((NT - b + GBUF - 1) // GBUF))
            gather(gtab, idx_rel, D, L)

        @block.scalar
        def _(act):
            act.dma_start(w_gat[:, :, 0:D], Ws.rearrange("l i o -> i l o")).then_inc(s_wg, 16)
            act.dma_start(wd_sb[:], Wd.rearrange("l i o -> i l o")).then_inc(s_wg, 16)
            act.dma_start(att_bc[:, 0], att_s.rearrange("l h c -> l (h c)").partition_broadcast(P)).then_inc(s_wg, 16)
            act.dma_start(att_bc[:, 1], att_d.rearrange("l h c -> l (h c)").partition_broadcast(P)).then_inc(s_wg, 16)
            act.dma_start(bias_gat[:], gat_b.rearrange("l d -> d l"), allow_slow_non_contiguous=True).then_inc(s_wg, 16)
            act.dma_start(wr_sb[:], Wr.rearrange("r i o -> i r o")).then_inc(s_w, 16)
            act.dma_start(relb_bc[:], rel_b.rearrange("r o -> (r o)").partition_broadcast(P)).then_inc(s_w, 16)
            act.dma_start(gw_bc[:], gate_w.rearrange("r o k -> (r o k)").partition_broadcast(P)).then_inc(s_w, 16)
            act.dma_start(gateb_bc[:], gate_b.rearrange("r k -> (r k)").partition_broadcast(P)).then_inc(s_w, 16)
            act.dma_start(loop_sb[:], loop_w).then_inc(s_w, 16)
            n_bodies, n_visits, tail = counts(act)
            for s, n in ((s_p, LAG), (s_pc, LAG_SUM)):
                act.sem_inc(s, n)

            def relu(t, b, code):
                act.wait_ge(s_sc, t)
                act.activation(relu4[:, b, :], ps_scores[b][:], ACT.Relu,
                               bias=ad4[:, bass.ds(window_of(act, code), 1)], scale=4.0).then_inc(s_relu, 1)

            def expo(t, k):
                b = k % 2
                act.wait_ge(s_max, t)
                act.activation(pt[:, b, :], nz[:, b, :], ACT.Exp, bias=nmax_new[:, b:b + 1], scale=-1.0)
                act.activation(fade[:, k:k + 1], nmax_old[:, k:k + 1], ACT.Exp, bias=nmax_new[:, b:b + 1],
                               scale=-1.0).then_inc(s_p, 1)

            def weights(t, b):
                act.wait_ge(s_pt, t)
                act.copy(pe_w[:, b].rearrange("p j m -> p (j m)"), ps_w[b][:]).then_inc(s_pc, 1)

            def visits(first, code, back, more):
                for k in range(U):
                    t = act.snap(first + (k + 2))
                    if back or k >= LAG:
                        weights(t, k % 2)
                    if more or k < U - 1:
                        relu(t, 1 - k % 2, code[k])
                    expo(t, k)

            with act.Fori(0, L) as l:
                for n, (bank, t, m) in enumerate(table_tiles()):
                    act.wait_ge(s_t, l * (2 * PARTS) + n + 1)
                    rows = bank[:, 0:m * (D + H)].rearrange("p (t c) -> p t c", t=m)
                    act.copy(stage[:, t:t + m, 0:D], rows[:, :, 0:D])
                    act.activation(stage[:, t:t + m, D + 1:RW], rows[:, :, D:D + H], ACT.Copy,
                                   scale=SHRINK).then_inc(s_tu, 1)
                stand(act, s_adu, (l + 1) * (2 * PARTS))
                base = l * n_visits
                code = codes(act, ENG.Activation, 0, U + 1)
                relu(base + 1, 0, code[0])
                visits(base, code[1:], False, True)
                with act.Fori(1, n_bodies - 1) as i:
                    visits(base + i * U, codes(act, ENG.Activation, i * U + 1, U), True, True)
                visits(base + tail, codes(act, ENG.Activation, tail + 1, U - 1), True, False)
                for b in range(LAG):
                    weights(base + n_visits + (b + 2), b)

            def roots(m):
                act.wait_ge(s_var, m + 1)
                part = rstd[:, (m % PARTS) * TP:(m % PARTS + 1) * TP]
                act.sqrt(part, part).then_inc(s_root, 1)

            roots(0)
            for n, (bank, t, m) in enumerate(table_tiles()):
                if n % 2 == 0 and n // 2 + 1 < PARTS:
                    roots(n // 2 + 1)
                act.wait_ge(s_x1, n + 1)
                act.copy(h_fm[:, t * P:(t + m) * P], bank[:, 0:m * P]).then_inc(s_x1u, 1)
            act.wait_ge(s_gz, 1)
            act.activation(ge[:], gz[:], ACT.Exp, scale=-1.0).then_inc(s_ge, 1)
            act.wait_ge(s_gate, 1)
            for t in range(NT):
                act.wait_ge(s_mu, t + 1)
                if t >= GBUF:
                    act.wait_ge(s_gt[t % GBUF], 16 * (t // GBUF))
                for r in range(R_DVE, NREL):
                    last = act.activation(gmsg[:, t % GBUF, r * D:(r + 1) * D], msg[:, t % 2, r * D:(r + 1) * D],
                                          ACT.Copy, scale=gate[:, t, r:r + 1])
                last.then_inc(s_gm, 1)
            for m in range(PARTS, 2 * PARTS):
                roots(m)

        @block.tensor
        def _(pe):
            pe.wait_ge(s_const, 2)
            n_set = 0

            def bank():
                nonlocal n_set
                if n_set >= 8:
                    pe.wait_ge(s_setf, n_set - 7)
                n_set += 1
                return ps[(n_set - 1) % 8]

            pe.wait_ge(s_xin, 32)
            for t0 in range(0, NT, 4):
                o = bank()
                for t in range(t0, min(t0 + 4, NT)):
                    last = pe.transpose(o[:, (t - t0) * P:(t - t0 + 1) * P], x_nm[:, t, :], ident[:])
                last.then_inc(s_set, 1)
            pe.wait_ge(s_lc, 1)
            o = bank()
            for k in range(4):
                last = pe.matmul(o[:, k * GR:(k + 1) * GR], lhsT=lo_cnt_x[:, k, :], rhs=ident[0:GR, 0:GR],
                                 start=True, stop=True)
            last.then_inc(s_set, 1)
            pe.wait_ge(s_rows, 1)
            for k in range(3):
                for r in range(2):
                    o = bank()
                    for j in range(J):
                        last = pe.transpose(o[:, j * GR:(j + 1) * GR], rows_f[k][:, r, j * P:(j + 1) * P],
                                            ident[0:GR, 0:GR])
                    last.then_inc(s_set, 1)
            n_bodies, n_visits, tail = counts(pe)
            pe.sem_inc(s_pt, LAG + 1)
            pe.sem_inc(s_sum, LAG_ADD)
            pe.wait_ge(s_setf, n_set)

            def scores(t, b):
                pe.wait_ge(s_mask, t)
                for j in range(J):
                    last = pe.transpose(ps_scores[b][:, j * P:(j + 1) * P], lmask[:, b, j, :], ident[:])
                last.then_inc(s_sc, 1)

            def turn(t, b):
                pe.wait_ge(s_p, t)
                for j in range(J):
                    last = pe.transpose(ps_w[b][:, j * P:(j + 1) * P], pt[:, b, j * P:(j + 1) * P], ident[:])
                last.then_inc(s_pt, 1)

            def sums(t, b, slot, weights, s_weights, width):
                pe.wait_ge(s_weights, t)
                for j in range(J):
                    last = pe.matmul(ps_sum[b][:, 0:width], lhsT=weights[:, b, j, :],
                                     rhs=ring_flat[:, bass.ds(slot * (J * RW) + j * RW, width)],
                                     start=(j == 0), stop=(j == J - 1))
                last.then_inc(s_sum, 1)

            def visits(first, code, back):
                for k in range(U):
                    t = pe.snap(first + (k + 1))
                    scores(t, k % 2)
                    if back or k >= LAG_SUM:
                        sums(t, (k - LAG_SUM) % 2, slot_of(pe, code[k - (0 if back else LAG_SUM)]), pe_w, s_pc, AW)
                    if back or k >= LAG:
                        turn(t, k % 2)

            with pe.Fori(0, L) as l:
                w = w_gat[:, bass.ds(l, 1), :].rearrange("p l o -> p (l o)")
                for n, (bank, t0, m) in enumerate(table_tiles()):
                    if n % 2 == 0:
                        pe.wait_ge(s_h, l * PARTS + n // 2 + 1)
                    if n >= 4:
                        pe.wait_ge(s_tu, l * (2 * PARTS) + n - 3)
                    for k in range(m):
                        t = t0 + k
                        last = pe.matmul(bank[:, k * (D + H):(k + 1) * (D + H)], lhsT=h_fm[:, t * P:(t + 1) * P],
                                         rhs=w, start=True, stop=True)
                    last.then_inc(s_t, 1)
                for n, (_, t0, m) in enumerate(table_tiles()):
                    if n >= 4:
                        pe.wait_ge(s_adu, l * (2 * PARTS) + n - 3)
                    pe.matmul(ps_target[n % 4][:, 0:m * P], lhsT=adx_now[:].rearrange("p h w -> p (h w)"),
                              rhs=h_fm[:, t0 * P:(t0 + m) * P], start=True, stop=True).then_inc(s_ad, 1)
                stand(pe, s_adu, (l + 1) * (2 * PARTS))
                base = l * n_visits
                visits(base, codes(pe, ENG.PE, 0, U - LAG_SUM), False)
                with pe.Fori(1, n_bodies) as i:
                    visits(base + i * U, codes(pe, ENG.PE, i * U - LAG_SUM, U), True)
                code = codes(pe, ENG.PE, tail + (U - LAG_SUM), LAG_SUM)
                for k in range(LAG_SUM):
                    t = pe.snap(base + n_visits + (k + 1))
                    stand(pe, s_added, l * LAG_SUM + (k + 1))
                    sums(t, (k - LAG_SUM) % 2, slot_of(pe, code[k]), pe_w, s_pc, AW)
                    if k < LAG:
                        turn(t, k)

            def result(n):
                _, t0, m = table_tiles()[n]
                if n % 2 == 0:
                    pe.wait_ge(s_h, L * PARTS + n // 2 + 1)
                if n >= 4:
                    pe.wait_ge(s_nu, n - 3)
                for k in range(m):
                    last = pe.transpose(ps_target[n % 4][:, k * P:(k + 1) * P],
                                        h_fm[:, (t0 + k) * P:(t0 + k + 1) * P], ident[:])
                last.then_inc(s_n, 1)

            def normed(n):
                bank, t0, m = table_tiles()[n]
                pe.wait_ge(s_norm, t0 + m)
                if n >= 4:
                    pe.wait_ge(s_x1u, n - 3)
                for k in range(m):
                    last = pe.transpose(bank[:, k * P:(k + 1) * P], x_nm[:, t0 + k, :], ident[:])
                last.then_inc(s_x1, 1)

            def gate_arguments(m):
                pe.wait_ge(s_x1u, 2 * m + 2)
                for t in range(m * TP, (m + 1) * TP):
                    last = pe.matmul(ps_gate[:, t * NREL:(t + 1) * NREL], lhsT=h_fm[:, t * P:(t + 1) * P],
                                     rhs=wg[:], start=True, stop=True)
                if m == PARTS - 1:
                    last.then_inc(s_g, 1)

            pe.wait_ge(s_folded, 1)
            for n in range(4):
                result(n)
            for n in range(2 * PARTS):
                if n + 4 < 2 * PARTS:
                    result(n + 4)
                normed(n)
                if n == 2 * PARTS - 3:
                    pe.wait_ge(s_nu, 2 * PARTS - 2)
                    for m in range(PARTS - 2):
                        gate_arguments(m)
            gate_arguments(PARTS - 2)
            gate_arguments(PARTS - 1)
            pe.wait_ge(s_x1u, 2 * PARTS)
            for t in range(NT):
                if t >= 2:
                    pe.wait_ge(s_mu, t - 1)
                for q in range(2):
                    last = pe.matmul(ps[2 * (t % 2) + q][:], lhsT=h_fm[:, t * P:(t + 1) * P],
                                     rhs=wr_sb[:, q * NREL // 2:(q + 1) * NREL // 2, :].rearrange("p r o -> p (r o)"),
                                     start=True, stop=True)
                last.then_inc(s_m, 1)
            base = n_visits * L
            pe.wait_ge(s_mu, NT)
            with pe.Fori(0, n_bodies) as i:
                code = codes(pe, ENG.PE, i * U, U)
                for k in range(U):
                    sums(pe.snap(base + i * U + (k + 1)), k % 2, slot_of(pe, code[k]), lmask, s_mask, D)
            for n, (_, t0, m) in enumerate(table_tiles()):
                if n % 2 == 0:
                    pe.wait_ge(s_h, (L + 1) * PARTS + n // 2 + 1)
                if n >= 4:
                    pe.wait_ge(s_nu, 2 * PARTS + n - 3)
                for k in range(m):
                    tile = slice((t0 + k) * P, (t0 + k + 1) * P)
                    o = ps_target[n % 4][:, k * P:(k + 1) * P]
                    pe.matmul(o, lhsT=h_fm[:, tile], rhs=loop_sb[:], start=True, stop=False)
                    last = pe.matmul(o, lhsT=diag_t[:, tile], rhs=ident[:], start=False, stop=True)
                last.then_inc(s_n, 1)

        @block.vector
        def _(dve):
            dve.sem_inc(s_max, 1)
            dve.memset(rows_i[0][:, 1, :], PAD_DST)
            dve.memset(rows_i[1][:, 1, :], 0)
            dve.memset(rows_i[2][:, 1, :], 0)
            dve.memset(x_nm[:, NT - 1, :], 0.0).then_inc(s_pad, 1)
            n_set = 0
            for t0 in range(0, NT, 4):
                m = min(4, NT - t0) * P
                dve.wait_ge(s_set, n_set + 1)
                dve.tensor_copy(h_fm[:, t0 * P:t0 * P + m], ps[n_set % 8][:, 0:m]).then_inc(s_setf, 1)
                n_set += 1
            def next_targets(l):
                dve.tensor_copy(adx_now[:], ad_w[:, bass.ds(l, 1), :].rearrange("p l h -> p (l h)")
                                .unsqueeze(2).to_broadcast([P, H, W]))

            dve.memset(ad_w[:, L, :], 0.0)
            dve.memset(relu_floor[:, 0:L - 1], 0.0)
            dve.memset(relu_floor[:, L - 1:L], -3.0e38)
            dve.memset(stage[:, :, D:D + 1], 1.0)
            dve.wait_ge(s_wg, 16 * 5)
            for l in range(L):
                for k, w, o in ((0, w_gat[:, l, 0:D], w_gat[:, l, D:D + H]), (1, wd_sb[:, l, :], ad_w[:, l, :])):
                    fold_l = fold[:, k * D:(k + 1) * D]
                    dve.tensor_tensor(fold_l, w, att_bc[:, k, l, :], ALU.mult)
                    dve.drain()
                    dve.tensor_reduce(o, fold_l.rearrange("p (h c) -> p h c", h=H), AX, ALU.add)
            dve.drain()
            next_targets(0)
            dve.drain()
            dve.sem_inc(s_h, PARTS)
            dve.sem_inc(s_read, PARTS)
            dve.wait_ge(s_edge, 16 * 9)
            for k in range(3):
                dve.tensor_copy(rows_f[k][:], rows_i[k][:])
            dve.drain()
            dve.scalar_tensor_tensor(rows_f[2][:], rows_f[1][:], float(NREL), rows_f[2][:], ALU.mult,
                                     ALU.add).then_inc(s_rows, 1)
            dve.tensor_reduce(mm[:, 0:2], rows_f[0][:], AX, ALU.min)
            dve.tensor_reduce(mm[:, 2:4], rows_f[0][:], AX, ALU.max)
            dve.drain()
            dve.tensor_copy(mmi[:], mm[:])
            dve.drain()
            dve.tensor_single_scalar(mmi[:], mmi[:], 5, ALU.arith_shift_right)
            dve.drain()
            dve.tensor_copy(lo_cnt[:], mmi[:])
            dve.drain()
            dve.scalar_tensor_tensor(lo_cnt[:, 2:4], lo_cnt[:, 2:4], 1.0, lo_cnt[:, 0:2], ALU.add, ALU.subtract)
            dve.drain()
            dve.tensor_copy(lo_cnt_x[:], lo_cnt[:].unsqueeze(2).to_broadcast([GR, 4, P])).then_inc(s_lc, 1)
            dve.memset(ones_g, 1.0)
            dve.memset(step_k, 128.0 + 32768.0)
            dve.drain()
            dve.memset(step_k.rearrange("p (i k) -> p i k", k=RING)[:, :, 0:1], 128.0 - 32768.0 * (RING - 1))
            dve.drain()
            dve.memset(step_k[:, 0:1], 0.0)
            dve.wait_ge(s_set, n_set + 1)
            low, cnt = (ps[n_set % 8][:, k * G:(k + 1) * G] for k in range(2))
            dve.tensor_tensor_scan(incl, ones_g, cnt, 0.0, ALU.mult, ALU.add)
            dve.drain()
            dve.tensor_tensor(off, incl, cnt, ALU.subtract)
            dve.drain()
            dve.tensor_tensor(gap, low, off, ALU.subtract).then_inc(s_setf, 1)
            n_set += 1
            dve.drain()
            dve.tensor_tensor(step_k[:, 1:G], step_k[:, 1:G], gap[:, 1:G], ALU.add)
            dve.tensor_copy(lead[:, 0:1], gap[:, 0:1])
            dve.drain()
            dve.tensor_tensor(step_k[:, 1:G], step_k[:, 1:G], gap[:, 0:G - 1], ALU.subtract)
            dve.tensor_tensor(step_k[:, 0:1], step_k[:, 0:1], lead[:, 0:1], ALU.add)
            dve.tensor_copy(incl_i[:], incl[0:1, :])
            dve.tensor_scalar(ctl_f[:], incl[0:1, G - 1:G], float(U - 1), None, ALU.add)
            dve.drain()
            dve.tensor_copy(ctl[:, 0:1], ctl_f[:])
            dve.drain()
            dve.tensor_single_scalar(ctl[:, 0:1], ctl[:, 0:1], U.bit_length() - 1, ALU.arith_shift_right)
            dve.drain()
            dve.tensor_single_scalar(ctl[:, 1:2], ctl[:, 0:1], U, ALU.mult)
            dve.drain()
            dve.tensor_single_scalar(ctl[:, 2:3], ctl[:, 1:2], VB, ALU.add)
            dve.tensor_copy(incl_i[:, G - 1:G], ctl[:, 1:2])
            dve.drain()
            dve.tensor_single_scalar(ctl[:, 2:3], ctl[:, 2:3], VB.bit_length() - 1, ALU.arith_shift_right)
            dve.drain()
            dve.tensor_single_scalar(ctl[:, 3:4], ctl[:, 1:2], -U, ALU.add).then_inc(s_ctl, 1)
            n_bodies, n_visits, tail = counts(dve)
            n_blocks = dve.value_load(ctl[0:1, 2:3], min_val=1, max_val=VMAX // VB)
            for target in (dst_e[:], idx_gat[:].rearrange("p (g j) -> p g j", j=J),
                           idx_rel[:].rearrange("p (g j) -> p g j", j=J)):
                for r in range(2):
                    dve.wait_ge(s_set, n_set + 1)
                    dve.tensor_copy(target[:, r * GR:(r + 1) * GR, :].rearrange("p g j -> p j g"),
                                    ps[n_set % 8][:, 0:J * GR].rearrange("p (j g) -> p j g", j=J)).then_inc(s_setf, 1)
                    n_set += 1
            dve.wait_ge(s_const, 4)
            dve.tensor_reduce(eye_w[:], ident[:].rearrange("p (h n) -> p n h", h=H), AX, ALU.add)
            dve.drain()

            with dve.Fori(0, n_blocks) as b:
                dve.tensor_tensor(vge, vnum[:].unsqueeze(2).to_broadcast([P, J, G]),
                                  off.unsqueeze(1).to_broadcast([P, J, G]), ALU.is_ge)
                dve.drain()
                dve.tensor_tensor(vwt, vge, step_k.unsqueeze(1).to_broadcast([P, J, G]), ALU.mult)
                dve.drain()
                dve.tensor_reduce(vsum, vwt, AX, ALU.add)
                dve.drain()
                dve.tensor_tensor(vcode[:], vsum, vnum[:], ALU.add).then_inc(s_code, 1)
                dve.drain()
                dve.tensor_scalar(vnum[:], vnum[:], float(VB), None, ALU.add)
                stand(dve, s_vis, b * 16 + 16)
                dve.drain()
            dve.nop().then_inc(s_ready, 1)
            dve.wait_ge(s_w, 16 * 5)
            dve.tensor_tensor(fold, wr_sb[:].rearrange("p r o -> p (r o)"), gw_bc[:], ALU.mult)
            dve.drain()
            dve.tensor_reduce(wg[:], fold.rearrange("p (r o) -> p r o", r=NREL), AX, ALU.add)
            dve.drain()
            dve.tensor_tensor(fold, relb_bc[:], gw_bc[:], ALU.mult)
            dve.drain()
            dve.tensor_reduce(gbias[:], fold.rearrange("p (r o) -> p r o", r=NREL), AX, ALU.add)
            dve.drain()
            dve.tensor_tensor(gbias[:], gbias[:], gateb_bc[:], ALU.add).then_inc(s_folded, 1)

            def rows_landed(group, l):
                dve.wait_ge(s_landed, group + (l * G + 1))

            def members(group, window, n_rep):
                d = dst_e[:].rearrange("p g j -> p (g j)")[:, bass.ds(group * J, J)]
                n = node_no[:, bass.ds(window * W, W)]
                if n_rep == 1:
                    return (d.unsqueeze(2).to_broadcast([P, J, W]), n.unsqueeze(1).to_broadcast([P, J, W]))
                return (d.unsqueeze(2).unsqueeze(3).to_broadcast([P, J, H, W]),
                        n.unsqueeze(1).unsqueeze(2).to_broadcast([P, J, H, W]))

            def mask_dist(b, code, l):
                group = group_of(dve, code)
                rows_landed(group, l)
                d, n = members(group, window_of(dve, code), 1)
                dve.tensor_tensor(dist[:, b], d, n, ALU.not_equal)

            def mask_scores(b, code):
                slot = slot_of(dve, code) * (J * RW)
                rows = ring_flat[:, bass.ds(slot, J * RW)].rearrange("p (j c) -> p j c", c=RW)[:, :, D + 1:RW]
                dve.tensor_tensor(lmask[:, b].rearrange("p j (h n) -> p j h n", h=H),
                                  rows.unsqueeze(3).to_broadcast([P, J, H, W]),
                                  dist[:, b].unsqueeze(2).to_broadcast([P, J, H, W]),
                                  ALU.subtract).then_inc(s_mask, 1)

            def add(t, k, code):
                b = (k - LAG_ADD) % 2
                dve.wait_ge(s_sum, t)
                s = acc[:, bass.ds(window_of(dve, code) * AW, AW)]
                return dve.scalar_tensor_tensor(s, s, fade[:, k:k + 1], ps_sum[b][:, 0:AW], ALU.mult, ALU.add)

            def keep_max(b, code):
                dve.tensor_copy(nmax[:, bass.ds(window_of(dve, code), 1)], nmax_new[:, b:b + 1])

            def step(t, k, old, last, code, ahead, l):
                b = k % 2
                if old is not None:
                    added = add(t, (k - LAG_ADD) % U, old)
                    if ahead is None:
                        added.then_inc(s_added, 1)
                if ahead is not None:
                    mask_dist(1 - b, ahead, l)
                if last is not None:
                    dve.drain()
                    keep_max(1 - b, last)
                dve.drain()
                dve.tensor_copy(nmax_old[:, k:k + 1], nmax[:, bass.ds(window_of(dve, code), 1)])
                dve.drain()
                if ahead is not None:
                    mask_scores(1 - b, ahead)
                stand(dve, s_relu, t)
                dve.tensor_tensor_reduce(nz[:, b, :], ps_scores[b][:], relu4[:, b, :], -SLOPE / SHRINK,
                                         nmax_old[:, k:k + 1], ALU.add, ALU.min,
                                         nmax_new[:, b:b + 1]).then_inc(s_max, 1)

            def visits(first, code, l, back, more):
                for k in range(U):
                    t = dve.snap(first + (k + 1))
                    step(t, k, code[k] if back or k >= LAG_ADD else None,
                         code[LAG_ADD + k - 1] if back or k >= 1 else None, code[LAG_ADD + k],
                         code[LAG_ADD + k + 1] if more or k < U - 1 else None, l)

            def layer_end(scaled, finish):
                def pick(m):
                    for h in range(H):
                        rows = slice(h * W, (h + 1) * W)
                        o = diag[rows, m * TP * P:(m + 1) * TP * P].rearrange("p (w c) -> p w c", c=C)
                        s = acc_w[rows, m * TP * H:(m + 1) * TP * H, h * C:(h + 1) * C]
                        if scaled:
                            r = rden[rows, m * TP * H:(m + 1) * TP * H].unsqueeze(2).to_broadcast([W, TP * H, C])
                            last = dve.tensor_tensor(o, s, r, ALU.mult)
                        else:
                            last = dve.tensor_copy(o, s)
                    last.then_inc(s_read, 1)

                def turned(m):
                    cols = slice(m * TP * P, (m + 1) * TP * P)
                    return dve.transpose(diag_t[:, cols], diag[:, cols])

                pick(0)
                for m in range(PARTS):
                    dve.drain()
                    last = turned(m)
                    if finish is None:
                        last.then_inc(s_h, 1)
                    if m < PARTS - 1:
                        pick(m + 1)
                    if finish is not None:
                        dve.drain()
                        finish(m)

            with dve.Fori(0, L) as l:
                for n, (_, t, m) in enumerate(table_tiles()):
                    dve.wait_ge(s_ad, l * (2 * PARTS) + n + 1)
                    picked = relu4[:, n % 2, 0:m * P].rearrange("p (w n) -> p w n", n=W)
                    dve.scalar_tensor_tensor(picked, ps_target[n % 4][:, 0:m * P].rearrange("p (w n) -> p w n", n=W),
                                             4.0 * SHRINK, eye_w[:].unsqueeze(1).to_broadcast([P, m * H, W]),
                                             ALU.mult, ALU.mult).then_inc(s_adu, 1)
                    dve.drain()
                    dve.tensor_reduce(ad4[:, t * H:(t + m) * H], picked, AX, ALU.add)
                next_targets(l + 1)
                dve.memset(nmax[:], FLOOR)
                dve.memset(ad4[:, NW:NWX], 0.0)
                stand(dve, s_zero, (l + 1) * PARTS)
                base = l * n_visits
                code = codes(dve, ENG.DVE, 0, U + 1)
                mask_dist(0, code[0], l)
                dve.drain()
                mask_scores(0, code[0])
                visits(base, (None,) * LAG_ADD + tuple(code), l, False, True)
                with dve.Fori(1, n_bodies - 1) as i:
                    visits(base + i * U, codes(dve, ENG.DVE, i * U - LAG_ADD, U + LAG_ADD + 1), l, True, True)
                code = codes(dve, ENG.DVE, tail - LAG_ADD, U + LAG_ADD)
                visits(base + tail, code, l, True, False)
                for k in range(LAG_ADD):
                    dve.drain()
                    added = add(base + n_visits + (k + 1), (k - LAG_ADD) % U, code[U + k])
                    if k < LAG_ADD - LAG:
                        added.then_inc(s_added, 1)
                dve.drain()
                dve.tensor_scalar(rden[:], acc_w[:, :, D:D + 1].rearrange("p w c -> p (w c)"), EPS_DEN, None, ALU.add)
                dve.drain()
                dve.reciprocal(rden[:], rden[:])
                dve.drain()


                def bias_relu(m):
                    cols = slice(m * TP * P, (m + 1) * TP * P)
                    dve.tensor_scalar(h_fm[:, cols], diag_t[:, cols], bias_gat[:, bass.ds(l, 1)],
                                      relu_floor[:, bass.ds(l, 1)], ALU.add, ALU.max).then_inc(s_h, 1)

                layer_end(True, bias_relu)

            def norm(first, relu_first):
                def stats(m):
                    for n in (2 * m, 2 * m + 1):
                        _, t, k = table_tiles()[n]
                        dve.wait_ge(s_n, 2 * first + n + 1)
                        new = ps_target[n % 4][:, 0:k * D]
                        x_part = x_nm[:, t:t + k, :].rearrange("p t d -> p (t d)")
                        if relu_first:
                            dve.scalar_tensor_tensor(x_part, new, 0.0, x_part, ALU.max, ALU.add).then_inc(s_nu, 1)
                        else:
                            dve.tensor_tensor(x_part, new, x_part, ALU.add).then_inc(s_nu, 1)
                    dve.drain()
                    part = slice(m * TP, (m + 1) * TP)
                    for t in range(m * TP, (m + 1) * TP):
                        dve.bn_stats(bn6[:, t, :], x_nm[:, t, :])
                    dve.drain()
                    for t in range(m * TP, (m + 1) * TP):
                        dve.bn_aggr(mv[:, t, :], bn6[:, t, :])
                    dve.drain()
                    dve.tensor_scalar(rstd[:, part], mv[:, part, 1], EPS_LN, None, ALU.add).then_inc(s_var, 1)

                def apply(m):
                    dve.wait_ge(s_root, first + m + 1)
                    dve.reciprocal(rstd[:, m * TP:(m + 1) * TP], rstd[:, m * TP:(m + 1) * TP])
                    dve.drain()
                    for t in range(m * TP, (m + 1) * TP):
                        dve.tensor_scalar(x_nm[:, t, :], x_nm[:, t, :], mv[:, t, 0:1], rstd[:, t:t + 1],
                                          ALU.subtract, ALU.mult).then_inc(s_norm, 1)

                for m in range(PARTS):
                    stats(m)
                    if m >= 1:
                        apply(m - 1)
                apply(PARTS - 1)

            norm(0, False)
            dve.wait_ge(s_g, 1)
            dve.tensor_tensor(gz[:], ps_gate[:, 0:NT * NREL].rearrange("p (t r) -> p t r", r=NREL),
                              gbias[:].unsqueeze(1).to_broadcast([P, NT, NREL]), ALU.add).then_inc(s_gz, 1)
            dve.wait_ge(s_ge, 1)
            dve.tensor_scalar(gate[:], ge[:], 1.0, None, ALU.add)
            dve.drain()
            dve.reciprocal(gate[:], gate[:]).then_inc(s_gate, 1)

            def gated(t):
                if t >= GBUF:
                    dve.wait_ge(s_gt[t % GBUF], 16 * (t // GBUF))
                dve.tensor_tensor(gmsg[:, t % GBUF, 0:R_DVE * D].rearrange("p (r d) -> p r d", r=R_DVE),
                                  msg[:, t % 2, 0:R_DVE * D].rearrange("p (r d) -> p r d", r=R_DVE),
                                  gate[:, t, 0:R_DVE].unsqueeze(2).to_broadcast([P, R_DVE, D]),
                                  ALU.mult).then_inc(s_gd, 1)

            for t in range(NT):
                dve.wait_ge(s_m, t + 1)
                if t >= 2:
                    dve.wait_ge(s_gm, t - 1)
                for q in range(2):
                    last = dve.tensor_tensor(msg[:, t % 2, q * 512:(q + 1) * 512], ps[2 * (t % 2) + q][:],
                                             relb_bc[:, q * 512:(q + 1) * 512], ALU.add)
                last.then_inc(s_mu, 1)
                if t >= 1:
                    gated(t - 1)
                dve.drain()
            gated(NT - 1)

            dve.wait_ge(s_zero, (L + 1) * PARTS)
            base = n_visits * L

            def match(b, code):
                group = group_of(dve, code)
                rows_landed(group, L)
                d, n = members(group, window_of(dve, code), H)
                dve.tensor_tensor(lmask[:, b].rearrange("p j (h n) -> p j h n", h=H), d, n,
                                  ALU.is_equal).then_inc(s_mask, 1)

            def add_plain(t, b, code):
                dve.wait_ge(s_sum, t)
                s = acc[:, bass.ds(window_of(dve, code) * AW, D)]
                dve.tensor_tensor(s, s, ps_sum[b][:, 0:D], ALU.add)

            code = codes(dve, ENG.DVE, 0, U)
            for k in range(U):
                if k >= LAG:
                    add_plain(base + (k + 1 - LAG + LAG_ADD), k % 2, code[k - LAG])
                match(k % 2, code[k])
                dve.drain()
            with dve.Fori(1, n_bodies) as i:
                code = codes(dve, ENG.DVE, i * U - LAG, U + LAG)
                for k in range(U):
                    add_plain(base + i * U + (k + 1 - LAG + LAG_ADD), k % 2, code[k])
                    match(k % 2, code[k + LAG])
                    dve.drain()
            code = codes(dve, ENG.DVE, tail + (U - LAG), LAG)
            for b in range(LAG):
                add_plain(base + n_visits + (b + 1 - LAG + LAG_ADD), b, code[b])
                dve.drain()
            layer_end(False, None)
            norm(PARTS, True)


_INS = ["x", "src", "dst", "edge_type_8", "L0_gnn_Ws", "L0_gnn_Wd", "L0_gnn_att_s", "L0_gnn_att_d", "L0_gnn_b",
        "L1_gnn_W", "L1_gnn_bias_term", "L1_gnn_gate_weight", "L1_gnn_gate_bias", "L1_gnn_loop_weight"]


def kernel(**inputs):
    import numpy as _np
    import concourse.bacc as _bacc
    from concourse import mybir as _mybir
    from concourse.bass_utils import run_bass_kernel_spmd as _run

    nc = _bacc.Bacc("TRN2", target_bir_lowering=False, num_devices=1)
    arrays, args = {}, []
    for name in _INS:
        a = _np.ascontiguousarray(inputs[name])
        arrays[f"in_{name}_dram"] = a
        args.append(nc.dram_tensor(f"in_{name}_dram", a.shape, _mybir.dt.from_np(a.dtype), kind="ExternalInput").ap())
    result = nc.dram_tensor("out_0_dram", (N, D), F32, kind="ExternalOutput").ap()
    build(nc, *args, result)
    r = _run(nc, [arrays], core_ids=[0])
    return r.results[0]["out_0_dram"]
```

```python
from contextlib import ExitStack

import concourse.bass as bass
from concourse import mybir

F32 = mybir.dt.float32
I32 = mybir.dt.int32
ALU = mybir.AluOpType
ACT = mybir.ActivationFunctionType
AX = mybir.AxisListType.X
ENG = mybir.EngineType

P = 128
N = 3125
E = 100000
D = 128
H = 4
C = D // H
L = 3
NREL = 8
SLOPE = 0.2
EPS_DEN = 1e-16
EPS_LN = 1e-5

W = P // H
J = 4
GE = J * P
GR = 98
G = 2 * GR
NT = (N + P - 1) // P
NP = NT * P
Q = 8
U = 2 * Q
PARTS = 5
TP = NT // PARTS
T0 = 3
GBUF = 4
R_DVE = 2
LAG = 2
LAG_SUM = 3
LAG_ADD = 4
NW = NP // W
PAD_DST = (N + W - 1) // W * W - 1
NWX = PAD_DST // W + Q
RING = 14
ITS = G // RING
HALF = RING // 2
LAG_FREE = 10
RW = D + 1 + H
AW = D + 1
SHRINK = 2.0 ** -64
FLOOR = 1e15
VB = 512
VMAX = G * (N // W + 1) + 2 * VB
assert RING * ITS == G and LAG_ADD <= Q and PARTS * TP == NT and T0 * RW <= 512 and PAD_DST < NP and NWX >= NW


def build(nc, x, src, dst, et, Ws, Wd, att_s, att_d, gat_b, Wr, rel_b, gate_w, gate_b, loop_w, out):
    with ExitStack() as ctx:
        def sb(name, shape, dt=F32):
            return ctx.enter_context(nc.sbuf_tensor(name, shape, dt))

        def sem(name):
            return ctx.enter_context(nc.semaphore(name))

        xtab = nc.dram_tensor("xtab", (NP, RW), F32).ap()
        gtab = nc.dram_tensor("gtab", (NP * NREL, D), F32).ap()
        vis = nc.dram_tensor("vis", (VMAX,), I32).ap()

        ident = sb("ident", [P, P])
        eye_w = sb("eye_w", [P, W])
        node_no = sb("node_no", [P, NWX * W])
        x_nm = sb("x_nm", [P, NT, D])
        h_fm = sb("h_fm", [P, NP])
        acc = sb("acc", [P, NWX * AW])
        ring = sb("ring", [P, RING, J, RW])
        stage = sb("stage", [P, NT, RW])
        dst_e = sb("dst_e", [P, G, J])
        idx_gat = sb("idx_gat", [P, G * J], I32)
        idx_rel = sb("idx_rel", [P, G * J], I32)
        idx_now = sb("idx_now", [P, 2, HALF * J], I32)
        w_gat = sb("w_gat", [P, L, D + H])
        wd_sb = sb("wd_sb", [P, L, D])
        ad_w = sb("ad_w", [P, L + 1, H])
        adx_now = sb("adx_now", [P, H, W])
        bias_gat = sb("bias_gat", [P, L])
        relu_floor = sb("relu_floor", [P, L])
        att_bc = sb("att_bc", [P, 2, L, D])
        ad4 = sb("ad4", [P, NWX])
        nmax = sb("nmax", [P, NWX])
        rden = sb("rden", [P, NW])
        dist = sb("dist", [P, 2, J, W])
        lmask = sb("lmask", [P, 2, J, P])
        relu4 = sb("relu4", [P, 2, GE])
        nz = sb("nz", [P, 2, GE])
        nmax_old = sb("nmax_old", [P, Q])
        nmax_new = sb("nmax_new", [P, 2])
        pt = sb("pt", [P, 2, GE])
        fade = sb("fade", [P, Q])
        pe_w = sb("pe_w", [P, 2, J, P])
        wr_sb = sb("wr_sb", [P, NREL, D])
        relb_bc = sb("relb_bc", [P, NREL * D])
        gw_bc = sb("gw_bc", [P, NREL * D])
        gateb_bc = sb("gateb_bc", [P, NREL])
        wg = sb("wg", [P, NREL])
        gbias = sb("gbias", [P, NREL])
        gz = sb("gz", [P, NT, NREL])
        ge = sb("ge", [P, NT, NREL])
        gate = sb("gate", [P, NT, NREL])
        loop_sb = sb("loop_sb", [P, D])
        bn6 = sb("bn6", [P, NT, 6])
        mv = sb("mv", [P, NT, 2])
        rstd = sb("rstd", [P, NT])
        vcode = sb("vcode", [P, J], I32)
        vnum = sb("vnum", [P, J])
        ctl_f = sb("ctl_f", [1, 1])
        ctl = sb("ctl", [1, 6], I32)
        incl_i = sb("incl_i", [1, G], I32)

        acc_w = acc[:].rearrange("p (w c) -> p w c", c=AW)
        ring_flat = ring[:].rearrange("p r j c -> p (r j c)")
        acc_w = acc_w[:, 0:NW, :]
        diag = ring_flat[:, 0:NP]
        diag_t = ring_flat[:, NP:2 * NP]
        msg = ring_flat[:, 0:2 * NREL * D].rearrange("p (b m) -> p b m", b=2)
        gmsg = ring_flat[:, 2 * NREL * D:(2 + GBUF) * NREL * D].rearrange("p (b m) -> p b m", b=GBUF)
        ring_i, ring_f = (ring_flat[0:GR, k * 3072:(k + 1) * 3072].rearrange("p (k r e) -> p k r e", k=3, r=2)
                          for k in range(2))
        rows_i = [ring_i[:, k].bitcast(I32) for k in range(3)]
        rows_f = [ring_f[:, k] for k in range(3)]
        mm = ring_flat[0:GR, 6144:6148]
        mmi = ring_flat[0:GR, 6148:6152].bitcast(I32)
        lo_cnt = ring_flat[0:GR, 6152:6156]
        lo_cnt_x = ring_flat[0:GR, 6156:6156 + 4 * P].rearrange("p (k m) -> p k m", k=4)
        vrow = ring_flat[:, 0:6 * G].rearrange("p (k g) -> p k g", k=6)
        ones_g, incl, off, gap, step_k, lead = (vrow[:, k, :] for k in range(6))
        vsum = ring_flat[:, 6 * G:6 * G + J]
        vge = nz[:].rearrange("p b e -> p (b e)")[:, 0:J * G].rearrange("p (q g) -> p q g", q=J)
        vwt = pt[:].rearrange("p b e -> p (b e)")[:, 0:J * G].rearrange("p (q g) -> p q g", q=J)
        fold = pe_w[:].rearrange("p b j m -> p (b j m)")

        ps = [ctx.enter_context(nc.psum_tensor(f"bank{i}", [P, 512], F32)) for i in range(8)]
        ps_scores, ps_w, ps_sum = ps[0:2], ps[2:4], ps[4:6]
        ps_table, ps_target, ps_gate = ps[0:4], ps[4:8], ps[7]

        s_const = sem("s_const")
        s_wg = sem("s_wg")
        s_w = sem("s_w")
        s_xin = sem("s_xin")
        s_edge = sem("s_edge")
        s_pad = sem("s_pad")
        s_rows = sem("s_rows")
        s_set = sem("s_set")
        s_setf = sem("s_setf")
        s_lc = sem("s_lc")
        s_ctl = sem("s_ctl")
        s_code = sem("s_code")
        s_vis = sem("s_vis")
        s_ready = sem("s_ready")
        s_folded = sem("s_folded")
        s_read = sem("s_read")
        s_h = sem("s_h")
        s_t = sem("s_t")
        s_tu = sem("s_tu")
        s_ad = sem("s_ad")
        s_adu = sem("s_adu")
        s_tab = sem("s_tab")
        s_zero = sem("s_zero")
        s_idx = sem("s_idx")
        s_row = [sem(f"s_row{k}") for k in range(RING)]
        s_landed = sem("s_landed")
        s_free = sem("s_free")
        s_p = sem("s_p")
        s_pt = sem("s_pt")
        s_pc = sem("s_pc")
        s_sum = sem("s_sum")
        s_summed = sem("s_summed")
        s_pick = sem("s_pick")
        s_added = sem("s_added")
        s_mask = sem("s_mask")
        s_sc = sem("s_sc")
        s_relu = sem("s_relu")
        s_max = sem("s_max")
        s_n = sem("s_n")
        s_nu = sem("s_nu")
        s_var = sem("s_var")
        s_root = sem("s_root")
        s_norm = sem("s_norm")
        s_x1 = sem("s_x1")
        s_x1u = sem("s_x1u")
        s_g = sem("s_g")
        s_m = sem("s_m")
        s_mu = sem("s_mu")
        s_gz = sem("s_gz")
        s_ge = sem("s_ge")
        s_gate = sem("s_gate")
        s_gm = sem("s_gm")
        s_gd = sem("s_gd")
        s_gt = [sem(f"s_gt{b}") for b in range(GBUF)]
        s_stood = sem("s_stood")
        s_out = sem("s_out")

        block = ctx.enter_context(nc.Block())
        edge_lists = (dst, src, et)
        full_rows = E // GE - GR
        tail = E - (GR + full_rows) * GE

        def stand(eng, s, value):
            eng.wait_ge(s, value)
            eng.sem_inc(s_stood, 1)

        def counts(eng):
            eng.wait_ge(s_ctl, 1)
            n_visits = eng.value_load(ctl[0:1, 1:2], min_val=G, max_val=VMAX)
            tail = eng.value_load(ctl[0:1, 3:4], min_val=G - Q, max_val=VMAX - 2 * U)
            return n_visits, tail

        def bodies(eng):
            return (eng.value_load(ctl[0:1, 0:1], min_val=G // Q, max_val=VMAX // Q),
                    eng.value_load(ctl[0:1, 4:5], min_val=2, max_val=3),
                    eng.value_load(ctl[0:1, 5:6], min_val=(G // Q - 4) // 2, max_val=VMAX // U - 4))

        def codes(eng, kind, first, n):
            _, got = nc.values_load_multi_w_load_instructions(
                vis[bass.ds(first, n)].rearrange("(a b) -> a b", a=1), engines=[kind], min_val=0,
                max_val=(RING << 15) - 1, skip_runtime_bounds_check_because="made on chip from slot, group and window")
            return got

        def table_tiles():
            return [(ps_table[(2 * m + k) % 4], m * TP + k * T0, (T0, TP - T0)[k]) for m in range(PARTS) for k in range(2)]

        MADE = "the codes are made on chip from slot, group and window numbers"

        def slot_of(eng, code):
            return nc.s_assert_within(code >> 15, 0, RING - 1, skip_runtime_bounds_check_because=MADE)

        def group_of(eng, code):
            return nc.s_assert_within((code >> 7) & 255, 0, G - 1, skip_runtime_bounds_check_because=MADE)

        def window_of(eng, code):
            return nc.s_assert_within(code & 127, 0, NWX - 1, skip_runtime_bounds_check_because=MADE)

        @block.sync
        def _(sp):
            for k, a in enumerate(edge_lists):
                sp.dma_start(rows_i[k][:, 0, :], a[0:GR * GE].rearrange("(p e) -> p e", e=GE)).then_inc(s_edge, 16)
            sp.wait_ge(s_pad, 1)
            nf = N // P
            sp.dma_start(x_nm[:, 0:nf, :], x[0:nf * P, :].rearrange("(t p) d -> p t d", p=P)).then_inc(s_xin, 16)
            sp.dma_start(x_nm[0:N - nf * P, nf, :], x[nf * P:N, :]).then_inc(s_xin, 16)
            for k, a in enumerate(edge_lists):
                sp.dma_start(rows_i[k][0:full_rows, 1, :],
                             a[GR * GE:(GR + full_rows) * GE].rearrange("(p e) -> p e", e=GE)).then_inc(s_edge, 16)
                sp.dma_start(rows_i[k][full_rows:GR, 1, 0:tail],
                             a[(GR + full_rows) * GE:E].rearrange("(p e) -> p e", p=1)).then_inc(s_edge, 16)
            sp.wait_ge(s_ctl, 1)
            n_blocks = sp.value_load(ctl[0:1, 2:3], min_val=1, max_val=VMAX // VB)
            n_visits, _ = counts(sp)
            with sp.Fori(0, n_blocks) as b:
                sp.wait_ge(s_code, b + 1)
                sp.dma_start(vis[bass.ds(b * VB, VB)].rearrange("(p q) -> p q", q=J), vcode[:]).then_inc(s_vis, 16)

            sp.sem_inc(s_free, RING)

            def follow(base, landed0, its0):
                def landed(it, k):
                    sp.wait_ge(s_row[k], (it + its0 + 1) * (16 * J))
                    sp.sem_inc(s_landed, 1)

                def free(g):
                    last = sp.value_load(incl_i[0:1, bass.ds(g, 1)], min_val=1, max_val=VMAX)
                    sp.wait_ge(s_sum, base + last + LAG_ADD)
                    sp.sem_inc(s_free, 1)

                for k in range(RING):
                    landed(0, k)
                    if k >= LAG_FREE:
                        free(k - LAG_FREE)
                with sp.Fori(1, ITS) as it:
                    for k in range(RING):
                        landed(it, k)
                        free(it * RING + (k - LAG_FREE))
                for g in range(G - LAG_FREE, G):
                    free(g)

            with sp.Fori(0, L) as l:
                for m in range(PARTS):
                    sp.wait_ge(s_tu, (l * PARTS + m + 1) * 2)
                    sp.dma_start(xtab[m * TP * P:(m + 1) * TP * P, :].rearrange("(t p) c -> p t c", p=P),
                                 stage[:, m * TP:(m + 1) * TP, :]).then_inc(s_tab, 16)
                follow(l * n_visits, l * G, l * ITS)
            for t in range(NT):
                sp.wait_ge(s_gm, t + 1)
                sp.wait_ge(s_gd, t + 1)
                sp.dma_start(gtab[t * P * NREL:(t + 1) * P * NREL, :].rearrange("(p r) d -> p (r d)", r=NREL),
                             gmsg[:, t % GBUF, :]).then_inc(s_gt[t % GBUF], 16)
            follow(n_visits * L, L * G, L * ITS)
            for t0 in range(0, nf, 6):
                t1 = min(t0 + 6, nf)
                sp.wait_ge(s_norm, NT + t1)
                sp.dma_start(out[t0 * P:t1 * P, :].rearrange("(t p) d -> p t d", p=P), x_nm[:, t0:t1, :]).then_inc(s_out, 16)
            sp.wait_ge(s_norm, 2 * NT)
            sp.dma_start(out[nf * P:N, :], x_nm[0:N - nf * P, nf, :]).then_inc(s_out, 16)
            sp.wait_ge(s_out, 16 * ((nf + 5) // 6 + 1))

        @block.gpsimd
        def _(pool):
            pool.memset(ident[:], 0.0).then_inc(s_const, 1)
            pool.wait_ge(s_const, 1)
            pool.affine_select(ident[:], ident[:], [[-1, P]], ALU.not_equal, 1.0, base=0,
                               channel_multiplier=1).then_inc(s_const, 1)
            pool.iota(node_no[:], [[1, NWX * W]], base=0, channel_multiplier=0,
                      allow_small_or_imprecise_dtypes=True).then_inc(s_const, 1)
            pool.iota(vnum[:], [[1, J]], base=0, channel_multiplier=J,
                      allow_small_or_imprecise_dtypes=True).then_inc(s_const, 1)

            def clear(l):
                for m in range(PARTS):
                    if isinstance(l, int):
                        pool.wait_ge(s_read, l * PARTS + m + 1)
                    else:
                        stand(pool, s_read, l * PARTS + m + 1)
                    end = NWX if m == PARTS - 1 else (m + 1) * TP * H
                    pool.memset(acc[:, m * TP * H * AW:end * AW], 0.0).then_inc(s_zero, 1)

            def gather(table, idx, width, l):
                with pool.Fori(0, ITS) as it:
                    for half in range(2):
                        pool.wait_ge(s_free, l * G + it * RING + (half * HALF + 1))
                        pool.tensor_copy(idx_now[:, half, :],
                                         idx[:, bass.ds(it * (RING * J) + half * HALF * J, HALF * J)]).then_inc(s_idx, 1)
                        pool.wait_ge(s_idx, (l * ITS + it) * 2 + half + 1)
                        for k in range(half * HALF, (half + 1) * HALF):
                            stand(pool, s_free, l * G + it * RING + (k + 1))
                            for j in range(J):
                                at = (k - half * HALF) * J + j
                                pool.indirect_dma_start(
                                    ring[:, k, j, 0:width], None, table,
                                    bass.IndirectOffsetOnAxis(idx_now[:, half, at:at + 1], 0)).then_inc(s_row[k], 16)

            with pool.Fori(0, L) as l:
                clear(l)
                pool.wait_ge(s_ready, 1)
                stand(pool, s_tab, (l + 1) * (16 * PARTS))
                gather(xtab, idx_gat, RW, l)
            clear(L)
            for b in range(GBUF):
                pool.wait_ge(s_gt[b], 16 * ((NT - b + GBUF - 1) // GBUF))
            gather(gtab, idx_rel, D, L)

        @block.scalar
        def _(act):
            act.dma_start(w_gat[:, :, 0:D], Ws.rearrange("l i o -> i l o")).then_inc(s_wg, 16)
            act.dma_start(wd_sb[:], Wd.rearrange("l i o -> i l o")).then_inc(s_wg, 16)
            act.dma_start(att_bc[:, 0], att_s.rearrange("l h c -> l (h c)").partition_broadcast(P)).then_inc(s_wg, 16)
            act.dma_start(att_bc[:, 1], att_d.rearrange("l h c -> l (h c)").partition_broadcast(P)).then_inc(s_wg, 16)
            act.dma_start(bias_gat[:], gat_b.rearrange("l d -> d l"), allow_slow_non_contiguous=True).then_inc(s_wg, 16)
            act.dma_start(wr_sb[:], Wr.rearrange("r i o -> i r o")).then_inc(s_w, 16)
            act.dma_start(relb_bc[:], rel_b.rearrange("r o -> (r o)").partition_broadcast(P)).then_inc(s_w, 16)
            act.dma_start(gw_bc[:], gate_w.rearrange("r o k -> (r o k)").partition_broadcast(P)).then_inc(s_w, 16)
            act.dma_start(gateb_bc[:], gate_b.rearrange("r k -> (r k)").partition_broadcast(P)).then_inc(s_w, 16)
            act.dma_start(loop_sb[:], loop_w).then_inc(s_w, 16)
            n_visits, tail = counts(act)
            _, n_lead, n_long = bodies(act)
            for s, n in ((s_p, LAG), (s_pc, LAG_SUM)):
                act.sem_inc(s, n)

            def pick():
                for m in range(PARTS):
                    for h in range(H // 2, H):
                        rows = slice(h * W, (h + 1) * W)
                        last = act.copy(diag[rows, m * TP * P:(m + 1) * TP * P].rearrange("p (w c) -> p w c", c=C),
                                        acc_w[rows, m * TP * H:(m + 1) * TP * H, h * C:(h + 1) * C])
                    last.then_inc(s_pick, 1)

            def relu(t, b, code):
                act.wait_ge(s_sc, t)
                act.activation(relu4[:, b, :], ps_scores[b][:], ACT.Relu,
                               bias=ad4[:, bass.ds(window_of(act, code), 1)], scale=4.0).then_inc(s_relu, 1)

            def expo(t, k):
                b, k = k % 2, k % Q
                act.wait_ge(s_max, t)
                act.activation(pt[:, b, :], nz[:, b, :], ACT.Exp, bias=nmax_new[:, b:b + 1], scale=-1.0)
                act.activation(fade[:, k:k + 1], nmax_old[:, k:k + 1], ACT.Exp, bias=nmax_new[:, b:b + 1],
                               scale=-1.0).then_inc(s_p, 1)

            def weights(t, b):
                act.wait_ge(s_pt, t)
                act.copy(pe_w[:, b].rearrange("p j m -> p (j m)"), ps_w[b][:]).then_inc(s_pc, 1)

            def visits(n, first, code, back=True, more=True):
                for k in range(n):
                    t = act.snap(first + (k + 2))
                    if back or k >= LAG:
                        weights(t, k % 2)
                    if more or k < n - 1:
                        relu(t, 1 - k % 2, code[k])
                    expo(t, k)

            with act.Fori(0, L) as l:
                for n, (bank, t, m) in enumerate(table_tiles()):
                    act.wait_ge(s_t, l * (2 * PARTS) + n + 1)
                    rows = bank[:, 0:m * (D + H)].rearrange("p (t c) -> p t c", t=m)
                    act.copy(stage[:, t:t + m, 0:D], rows[:, :, 0:D])
                    act.activation(stage[:, t:t + m, D + 1:RW], rows[:, :, D:D + H], ACT.Copy,
                                   scale=SHRINK).then_inc(s_tu, 1)
                stand(act, s_adu, (l + 1) * (2 * PARTS))
                base = l * n_visits
                code = codes(act, ENG.Activation, 0, Q + 1)
                relu(base + 1, 0, code[0])
                visits(Q, base, code[1:], back=False)
                with act.Fori(1, n_lead) as i:
                    visits(Q, base + i * Q, codes(act, ENG.Activation, i * Q + 1, Q))
                with act.Fori(0, n_long) as i:
                    first = act.snap(n_lead * Q + i * U)
                    visits(U, base + first, codes(act, ENG.Activation, first + 1, U))
                visits(Q, base + tail, codes(act, ENG.Activation, tail + 1, Q - 1), more=False)
                for b in range(LAG):
                    weights(base + n_visits + (b + 2), b)
                stand(act, s_summed, l + 1)
                pick()

            def roots(m):
                act.wait_ge(s_var, m + 1)
                part = rstd[:, (m % PARTS) * TP:(m % PARTS + 1) * TP]
                act.sqrt(part, part).then_inc(s_root, 1)

            roots(0)
            for n, (bank, t, m) in enumerate(table_tiles()):
                if n % 2 == 0 and n // 2 + 1 < PARTS:
                    roots(n // 2 + 1)
                act.wait_ge(s_x1, n + 1)
                act.copy(h_fm[:, t * P:(t + m) * P], bank[:, 0:m * P]).then_inc(s_x1u, 1)
            act.wait_ge(s_gz, 1)
            act.activation(ge[:], gz[:], ACT.Exp, scale=-1.0).then_inc(s_ge, 1)
            act.wait_ge(s_gate, 1)
            for t in range(NT):
                act.wait_ge(s_mu, t + 1)
                if t >= GBUF:
                    act.wait_ge(s_gt[t % GBUF], 16 * (t // GBUF))
                for r in range(R_DVE, NREL):
                    last = act.activation(gmsg[:, t % GBUF, r * D:(r + 1) * D], msg[:, t % 2, r * D:(r + 1) * D],
                                          ACT.Copy, scale=gate[:, t, r:r + 1])
                last.then_inc(s_gm, 1)
            act.wait_ge(s_summed, L + 1)
            pick()
            for m in range(PARTS, 2 * PARTS):
                roots(m)

        @block.tensor
        def _(pe):
            pe.wait_ge(s_const, 2)
            n_set = 0

            def bank():
                nonlocal n_set
                if n_set >= 8:
                    pe.wait_ge(s_setf, n_set - 7)
                n_set += 1
                return ps[(n_set - 1) % 8]

            pe.wait_ge(s_xin, 32)
            for t0 in range(0, NT, 4):
                o = bank()
                for t in range(t0, min(t0 + 4, NT)):
                    last = pe.transpose(o[:, (t - t0) * P:(t - t0 + 1) * P], x_nm[:, t, :], ident[:])
                last.then_inc(s_set, 1)
            pe.wait_ge(s_lc, 1)
            o = bank()
            for k in range(4):
                last = pe.matmul(o[:, k * GR:(k + 1) * GR], lhsT=lo_cnt_x[:, k, :], rhs=ident[0:GR, 0:GR],
                                 start=True, stop=True)
            last.then_inc(s_set, 1)
            pe.wait_ge(s_rows, 1)
            for k in range(3):
                for r in range(2):
                    o = bank()
                    for j in range(J):
                        last = pe.transpose(o[:, j * GR:(j + 1) * GR], rows_f[k][:, r, j * P:(j + 1) * P],
                                            ident[0:GR, 0:GR])
                    last.then_inc(s_set, 1)
            n_visits, tail = counts(pe)
            n_short, n_lead, n_long = bodies(pe)
            pe.sem_inc(s_pt, LAG + 1)
            pe.sem_inc(s_sum, LAG_ADD)
            pe.wait_ge(s_setf, n_set)

            def scores(t, b):
                pe.wait_ge(s_mask, t)
                for j in range(J):
                    last = pe.transpose(ps_scores[b][:, j * P:(j + 1) * P], lmask[:, b, j, :], ident[:])
                last.then_inc(s_sc, 1)

            def turn(t, b):
                pe.wait_ge(s_p, t)
                for j in range(J):
                    last = pe.transpose(ps_w[b][:, j * P:(j + 1) * P], pt[:, b, j * P:(j + 1) * P], ident[:])
                last.then_inc(s_pt, 1)

            def sums(t, b, slot, weights, s_weights, width):
                pe.wait_ge(s_weights, t)
                for j in range(J):
                    last = pe.matmul(ps_sum[b][:, 0:width], lhsT=weights[:, b, j, :],
                                     rhs=ring_flat[:, bass.ds(slot * (J * RW) + j * RW, width)],
                                     start=(j == 0), stop=(j == J - 1))
                last.then_inc(s_sum, 1)

            def visits(n, first, code, back=True):
                for k in range(n):
                    t = pe.snap(first + (k + 1))
                    scores(t, k % 2)
                    if back or k >= LAG_SUM:
                        sums(t, (k - LAG_SUM) % 2, slot_of(pe, code[k - (0 if back else LAG_SUM)]), pe_w, s_pc, AW)
                    if back or k >= LAG:
                        turn(t, k % 2)

            with pe.Fori(0, L) as l:
                w = w_gat[:, bass.ds(l, 1), :].rearrange("p l o -> p (l o)")
                for n, (bank, t0, m) in enumerate(table_tiles()):
                    if n % 2 == 0:
                        pe.wait_ge(s_h, l * PARTS + n // 2 + 1)
                    if n >= 4:
                        pe.wait_ge(s_tu, l * (2 * PARTS) + n - 3)
                    for k in range(m):
                        t = t0 + k
                        last = pe.matmul(bank[:, k * (D + H):(k + 1) * (D + H)], lhsT=h_fm[:, t * P:(t + 1) * P],
                                         rhs=w, start=True, stop=True)
                    last.then_inc(s_t, 1)
                for n, (_, t0, m) in enumerate(table_tiles()):
                    if n >= 4:
                        pe.wait_ge(s_adu, l * (2 * PARTS) + n - 3)
                    pe.matmul(ps_target[n % 4][:, 0:m * P], lhsT=adx_now[:].rearrange("p h w -> p (h w)"),
                              rhs=h_fm[:, t0 * P:(t0 + m) * P], start=True, stop=True).then_inc(s_ad, 1)
                stand(pe, s_adu, (l + 1) * (2 * PARTS))
                base = l * n_visits
                visits(Q, base, codes(pe, ENG.PE, 0, Q - LAG_SUM), back=False)
                with pe.Fori(1, n_lead) as i:
                    visits(Q, base + i * Q, codes(pe, ENG.PE, i * Q - LAG_SUM, Q))
                with pe.Fori(0, n_long) as i:
                    first = pe.snap(n_lead * Q + i * U)
                    visits(U, base + first, codes(pe, ENG.PE, first - LAG_SUM, U))
                code = codes(pe, ENG.PE, tail - LAG_SUM, Q + LAG_SUM)
                visits(Q, base + tail, code[0:Q])
                code = code[Q:]
                for k in range(LAG_SUM):
                    t = pe.snap(base + n_visits + (k + 1))
                    stand(pe, s_added, l * LAG_SUM + (k + 1))
                    sums(t, (k - LAG_SUM) % 2, slot_of(pe, code[k]), pe_w, s_pc, AW)
                    if k < LAG:
                        turn(t, k)

            def result(n):
                _, t0, m = table_tiles()[n]
                if n % 2 == 0:
                    pe.wait_ge(s_h, L * PARTS + n // 2 + 1)
                if n >= 4:
                    pe.wait_ge(s_nu, n - 3)
                for k in range(m):
                    last = pe.transpose(ps_target[n % 4][:, k * P:(k + 1) * P],
                                        h_fm[:, (t0 + k) * P:(t0 + k + 1) * P], ident[:])
                last.then_inc(s_n, 1)

            def normed(n):
                bank, t0, m = table_tiles()[n]
                pe.wait_ge(s_norm, t0 + m)
                if n >= 4:
                    pe.wait_ge(s_x1u, n - 3)
                for k in range(m):
                    last = pe.transpose(bank[:, k * P:(k + 1) * P], x_nm[:, t0 + k, :], ident[:])
                last.then_inc(s_x1, 1)

            def gate_arguments(m):
                pe.wait_ge(s_x1u, 2 * m + 2)
                for t in range(m * TP, (m + 1) * TP):
                    last = pe.matmul(ps_gate[:, t * NREL:(t + 1) * NREL], lhsT=h_fm[:, t * P:(t + 1) * P],
                                     rhs=wg[:], start=True, stop=True)
                if m == PARTS - 1:
                    last.then_inc(s_g, 1)

            pe.wait_ge(s_folded, 1)
            for n in range(4):
                result(n)
            for n in range(2 * PARTS):
                if n + 4 < 2 * PARTS:
                    result(n + 4)
                normed(n)
            pe.wait_ge(s_nu, 2 * PARTS)
            for m in range(PARTS):
                gate_arguments(m)
            pe.wait_ge(s_x1u, 2 * PARTS)
            for t in range(NT):
                if t >= 2:
                    pe.wait_ge(s_mu, t - 1)
                for q in range(2):
                    last = pe.matmul(ps[2 * (t % 2) + q][:], lhsT=h_fm[:, t * P:(t + 1) * P],
                                     rhs=wr_sb[:, q * NREL // 2:(q + 1) * NREL // 2, :].rearrange("p r o -> p (r o)"),
                                     start=True, stop=True)
                last.then_inc(s_m, 1)
            base = n_visits * L
            pe.wait_ge(s_mu, NT)
            with pe.Fori(0, n_short) as i:
                code = codes(pe, ENG.PE, i * Q, Q)
                for k in range(Q):
                    sums(pe.snap(base + i * Q + (k + 1)), k % 2, slot_of(pe, code[k]), lmask, s_mask, D)
            for n, (_, t0, m) in enumerate(table_tiles()):
                if n % 2 == 0:
                    pe.wait_ge(s_h, (L + 1) * PARTS + n // 2 + 1)
                if n >= 4:
                    pe.wait_ge(s_nu, 2 * PARTS + n - 3)
                for k in range(m):
                    tile = slice((t0 + k) * P, (t0 + k + 1) * P)
                    o = ps_target[n % 4][:, k * P:(k + 1) * P]
                    pe.matmul(o, lhsT=h_fm[:, tile], rhs=loop_sb[:], start=True, stop=False)
                    last = pe.matmul(o, lhsT=diag_t[:, tile], rhs=ident[:], start=False, stop=True)
                last.then_inc(s_n, 1)

        @block.vector
        def _(dve):
            dve.sem_inc(s_max, 1)
            dve.memset(rows_i[0][:, 1, :], PAD_DST)
            dve.memset(rows_i[1][:, 1, :], 0)
            dve.memset(rows_i[2][:, 1, :], 0)
            dve.memset(x_nm[:, NT - 1, :], 0.0).then_inc(s_pad, 1)
            n_set = 0
            for t0 in range(0, NT, 4):
                m = min(4, NT - t0) * P
                dve.wait_ge(s_set, n_set + 1)
                dve.tensor_copy(h_fm[:, t0 * P:t0 * P + m], ps[n_set % 8][:, 0:m]).then_inc(s_setf, 1)
                n_set += 1
            def next_targets(l):
                dve.tensor_copy(adx_now[:], ad_w[:, bass.ds(l, 1), :].rearrange("p l h -> p (l h)")
                                .unsqueeze(2).to_broadcast([P, H, W]))

            dve.memset(ad_w[:, L, :], 0.0)
            dve.memset(relu_floor[:, 0:L - 1], 0.0)
            dve.memset(relu_floor[:, L - 1:L], -3.0e38)
            dve.memset(stage[:, :, D:D + 1], 1.0)
            dve.wait_ge(s_wg, 16 * 5)
            for l in range(L):
                for k, w, o in ((0, w_gat[:, l, 0:D], w_gat[:, l, D:D + H]), (1, wd_sb[:, l, :], ad_w[:, l, :])):
                    fold_l = fold[:, k * D:(k + 1) * D]
                    dve.tensor_tensor(fold_l, w, att_bc[:, k, l, :], ALU.mult)
                    dve.drain()
                    dve.tensor_reduce(o, fold_l.rearrange("p (h c) -> p h c", h=H), AX, ALU.add)
            dve.drain()
            next_targets(0)
            dve.drain()
            dve.sem_inc(s_h, PARTS)
            dve.sem_inc(s_read, PARTS)
            dve.wait_ge(s_edge, 16 * 9)
            for k in range(3):
                dve.tensor_copy(rows_f[k][:], rows_i[k][:])
            dve.drain()
            dve.scalar_tensor_tensor(rows_f[2][:], rows_f[1][:], float(NREL), rows_f[2][:], ALU.mult,
                                     ALU.add).then_inc(s_rows, 1)
            dve.tensor_reduce(mm[:, 0:2], rows_f[0][:], AX, ALU.min)
            dve.tensor_reduce(mm[:, 2:4], rows_f[0][:], AX, ALU.max)
            dve.drain()
            dve.tensor_copy(mmi[:], mm[:])
            dve.drain()
            dve.tensor_single_scalar(mmi[:], mmi[:], 5, ALU.arith_shift_right)
            dve.drain()
            dve.tensor_copy(lo_cnt[:], mmi[:])
            dve.drain()
            dve.scalar_tensor_tensor(lo_cnt[:, 2:4], lo_cnt[:, 2:4], 1.0, lo_cnt[:, 0:2], ALU.add, ALU.subtract)
            dve.drain()
            dve.tensor_copy(lo_cnt_x[:], lo_cnt[:].unsqueeze(2).to_broadcast([GR, 4, P])).then_inc(s_lc, 1)
            dve.memset(ones_g, 1.0)
            dve.memset(step_k, 128.0 + 32768.0)
            dve.drain()
            dve.memset(step_k.rearrange("p (i k) -> p i k", k=RING)[:, :, 0:1], 128.0 - 32768.0 * (RING - 1))
            dve.drain()
            dve.memset(step_k[:, 0:1], 0.0)
            dve.wait_ge(s_set, n_set + 1)
            low, cnt = (ps[n_set % 8][:, k * G:(k + 1) * G] for k in range(2))
            dve.tensor_tensor_scan(incl, ones_g, cnt, 0.0, ALU.mult, ALU.add)
            dve.drain()
            dve.tensor_tensor(off, incl, cnt, ALU.subtract)
            dve.drain()
            dve.tensor_tensor(gap, low, off, ALU.subtract).then_inc(s_setf, 1)
            n_set += 1
            dve.drain()
            dve.tensor_tensor(step_k[:, 1:G], step_k[:, 1:G], gap[:, 1:G], ALU.add)
            dve.tensor_copy(lead[:, 0:1], gap[:, 0:1])
            dve.drain()
            dve.tensor_tensor(step_k[:, 1:G], step_k[:, 1:G], gap[:, 0:G - 1], ALU.subtract)
            dve.tensor_tensor(step_k[:, 0:1], step_k[:, 0:1], lead[:, 0:1], ALU.add)
            dve.tensor_copy(incl_i[:], incl[0:1, :])
            dve.tensor_scalar(ctl_f[:], incl[0:1, G - 1:G], float(Q - 1), None, ALU.add)
            dve.drain()
            dve.tensor_copy(ctl[:, 0:1], ctl_f[:])
            dve.drain()
            dve.tensor_single_scalar(ctl[:, 0:1], ctl[:, 0:1], Q.bit_length() - 1, ALU.arith_shift_right)
            dve.drain()
            dve.tensor_single_scalar(ctl[:, 1:2], ctl[:, 0:1], Q, ALU.mult)
            dve.tensor_single_scalar(ctl[:, 5:6], ctl[:, 0:1], -3, ALU.add)
            dve.drain()
            dve.tensor_single_scalar(ctl[:, 5:6], ctl[:, 5:6], 1, ALU.arith_shift_right)
            dve.drain()
            dve.tensor_single_scalar(ctl[:, 4:5], ctl[:, 5:6], -2, ALU.mult)
            dve.drain()
            dve.tensor_tensor(ctl[:, 4:5], ctl[:, 4:5], ctl[:, 0:1], ALU.add)
            dve.drain()
            dve.tensor_single_scalar(ctl[:, 4:5], ctl[:, 4:5], -1, ALU.add)
            dve.drain()
            dve.tensor_single_scalar(ctl[:, 2:3], ctl[:, 1:2], VB, ALU.add)
            dve.tensor_copy(incl_i[:, G - 1:G], ctl[:, 1:2])
            dve.drain()
            dve.tensor_single_scalar(ctl[:, 2:3], ctl[:, 2:3], VB.bit_length() - 1, ALU.arith_shift_right)
            dve.drain()
            dve.tensor_single_scalar(ctl[:, 3:4], ctl[:, 1:2], -Q, ALU.add).then_inc(s_ctl, 1)
            n_visits, tail = counts(dve)
            n_short, n_lead, n_long = bodies(dve)
            n_blocks = dve.value_load(ctl[0:1, 2:3], min_val=1, max_val=VMAX // VB)
            for target in (dst_e[:], idx_gat[:].rearrange("p (g j) -> p g j", j=J),
                           idx_rel[:].rearrange("p (g j) -> p g j", j=J)):
                for r in range(2):
                    dve.wait_ge(s_set, n_set + 1)
                    dve.tensor_copy(target[:, r * GR:(r + 1) * GR, :].rearrange("p g j -> p j g"),
                                    ps[n_set % 8][:, 0:J * GR].rearrange("p (j g) -> p j g", j=J)).then_inc(s_setf, 1)
                    n_set += 1
            dve.wait_ge(s_const, 4)
            dve.tensor_reduce(eye_w[:], ident[:].rearrange("p (h n) -> p n h", h=H), AX, ALU.add)
            dve.drain()

            with dve.Fori(0, n_blocks) as b:
                dve.tensor_tensor(vge, vnum[:].unsqueeze(2).to_broadcast([P, J, G]),
                                  off.unsqueeze(1).to_broadcast([P, J, G]), ALU.is_ge)
                dve.drain()
                dve.tensor_tensor(vwt, vge, step_k.unsqueeze(1).to_broadcast([P, J, G]), ALU.mult)
                dve.drain()
                dve.tensor_reduce(vsum, vwt, AX, ALU.add)
                dve.drain()
                dve.tensor_tensor(vcode[:], vsum, vnum[:], ALU.add).then_inc(s_code, 1)
                dve.drain()
                dve.tensor_scalar(vnum[:], vnum[:], float(VB), None, ALU.add)
                stand(dve, s_vis, b * 16 + 16)
                dve.drain()
            dve.nop().then_inc(s_ready, 1)
            dve.wait_ge(s_w, 16 * 5)
            dve.tensor_tensor(fold, wr_sb[:].rearrange("p r o -> p (r o)"), gw_bc[:], ALU.mult)
            dve.drain()
            dve.tensor_reduce(wg[:], fold.rearrange("p (r o) -> p r o", r=NREL), AX, ALU.add)
            dve.drain()
            dve.tensor_tensor(fold, relb_bc[:], gw_bc[:], ALU.mult)
            dve.drain()
            dve.tensor_reduce(gbias[:], fold.rearrange("p (r o) -> p r o", r=NREL), AX, ALU.add)
            dve.drain()
            dve.tensor_tensor(gbias[:], gbias[:], gateb_bc[:], ALU.add).then_inc(s_folded, 1)

            def rows_landed(group, l):
                dve.wait_ge(s_landed, group + (l * G + 1))

            def members(group, window, n_rep):
                d = dst_e[:].rearrange("p g j -> p (g j)")[:, bass.ds(group * J, J)]
                n = node_no[:, bass.ds(window * W, W)]
                if n_rep == 1:
                    return (d.unsqueeze(2).to_broadcast([P, J, W]), n.unsqueeze(1).to_broadcast([P, J, W]))
                return (d.unsqueeze(2).unsqueeze(3).to_broadcast([P, J, H, W]),
                        n.unsqueeze(1).unsqueeze(2).to_broadcast([P, J, H, W]))

            def mask_dist(b, code, l):
                group = group_of(dve, code)
                rows_landed(group, l)
                d, n = members(group, window_of(dve, code), 1)
                dve.tensor_tensor(dist[:, b], d, n, ALU.not_equal)

            def mask_scores(b, code):
                slot = slot_of(dve, code) * (J * RW)
                rows = ring_flat[:, bass.ds(slot, J * RW)].rearrange("p (j c) -> p j c", c=RW)[:, :, D + 1:RW]
                dve.tensor_tensor(lmask[:, b].rearrange("p j (h n) -> p j h n", h=H),
                                  rows.unsqueeze(3).to_broadcast([P, J, H, W]),
                                  dist[:, b].unsqueeze(2).to_broadcast([P, J, H, W]),
                                  ALU.subtract).then_inc(s_mask, 1)

            def add(t, k, code):
                b, k = (k - LAG_ADD) % 2, (k - LAG_ADD) % Q
                dve.wait_ge(s_sum, t)
                s = acc[:, bass.ds(window_of(dve, code) * AW, AW)]
                return dve.scalar_tensor_tensor(s, s, fade[:, k:k + 1], ps_sum[b][:, 0:AW], ALU.mult, ALU.add)

            def keep_max(b, code):
                dve.tensor_copy(nmax[:, bass.ds(window_of(dve, code), 1)], nmax_new[:, b:b + 1])

            def step(t, k, old, last, code, ahead, l):
                b, k = k % 2, k % Q
                if old is not None:
                    added = add(t, k, old)
                    if ahead is None:
                        added.then_inc(s_added, 1)
                if ahead is not None:
                    mask_dist(1 - b, ahead, l)
                if last is not None:
                    dve.drain()
                    keep_max(1 - b, last)
                dve.drain()
                dve.tensor_copy(nmax_old[:, k:k + 1], nmax[:, bass.ds(window_of(dve, code), 1)])
                dve.drain()
                if ahead is not None:
                    mask_scores(1 - b, ahead)
                stand(dve, s_relu, t)
                dve.tensor_tensor_reduce(nz[:, b, :], ps_scores[b][:], relu4[:, b, :], -SLOPE / SHRINK,
                                         nmax_old[:, k:k + 1], ALU.add, ALU.min,
                                         nmax_new[:, b:b + 1]).then_inc(s_max, 1)

            def visits(n, first, code, l, back=True, more=True):
                for k in range(n):
                    t = dve.snap(first + (k + 1))
                    step(t, k, code[k] if back or k >= LAG_ADD else None,
                         code[LAG_ADD + k - 1] if back or k >= 1 else None, code[LAG_ADD + k],
                         code[LAG_ADD + k + 1] if more or k < n - 1 else None, l)

            def layer_end(picked, scaled, finish):
                def columns(m, h0, h1):
                    rows = slice(h0 * W, h1 * W)
                    o = diag[rows, m * TP * P:(m + 1) * TP * P].rearrange("p (w c) -> p w c", c=C)
                    r = rden[rows, m * TP * H:(m + 1) * TP * H].unsqueeze(2).to_broadcast([(h1 - h0) * W, TP * H, C])
                    return rows, o, r

                def pick(m):
                    for h in range(H // 2):
                        rows, o, r = columns(m, h, h + 1)
                        s = acc_w[rows, m * TP * H:(m + 1) * TP * H, h * C:(h + 1) * C]
                        if scaled:
                            dve.tensor_tensor(o, s, r, ALU.mult)
                        else:
                            dve.tensor_copy(o, s)
                    picked(m + 1)
                    if scaled:
                        _, o, r = columns(m, H // 2, H)
                        dve.tensor_tensor(o, o, r, ALU.mult).then_inc(s_read, 1)

                def turned(m):
                    cols = slice(m * TP * P, (m + 1) * TP * P)
                    return dve.transpose(diag_t[:, cols], diag[:, cols])

                pick(0)
                for m in range(PARTS):
                    dve.drain()
                    last = turned(m)
                    if finish is None:
                        last.then_inc(s_h, 1)
                    if m < PARTS - 1:
                        pick(m + 1)
                    if finish is not None:
                        dve.drain()
                        finish(m)

            with dve.Fori(0, L) as l:
                for n, (_, t, m) in enumerate(table_tiles()):
                    dve.wait_ge(s_ad, l * (2 * PARTS) + n + 1)
                    picked = relu4[:, n % 2, 0:m * P].rearrange("p (w n) -> p w n", n=W)
                    dve.scalar_tensor_tensor(picked, ps_target[n % 4][:, 0:m * P].rearrange("p (w n) -> p w n", n=W),
                                             4.0 * SHRINK, eye_w[:].unsqueeze(1).to_broadcast([P, m * H, W]),
                                             ALU.mult, ALU.mult).then_inc(s_adu, 1)
                    dve.drain()
                    dve.tensor_reduce(ad4[:, t * H:(t + m) * H], picked, AX, ALU.add)
                next_targets(l + 1)
                dve.memset(nmax[:], FLOOR)
                dve.memset(ad4[:, NW:NWX], 0.0)
                stand(dve, s_zero, (l + 1) * PARTS)
                base = l * n_visits
                code = codes(dve, ENG.DVE, 0, Q + 1)
                mask_dist(0, code[0], l)
                dve.drain()
                mask_scores(0, code[0])
                visits(Q, base, (None,) * LAG_ADD + tuple(code), l, back=False)
                with dve.Fori(1, n_lead) as i:
                    visits(Q, base + i * Q, codes(dve, ENG.DVE, i * Q - LAG_ADD, Q + LAG_ADD + 1), l)
                with dve.Fori(0, n_long) as i:
                    first = dve.snap(n_lead * Q + i * U)
                    visits(U, base + first, codes(dve, ENG.DVE, first - LAG_ADD, U + LAG_ADD + 1), l)
                code = codes(dve, ENG.DVE, tail - LAG_ADD, Q + LAG_ADD)
                visits(Q, base + tail, code, l, more=False)
                for k in range(LAG_ADD):
                    dve.drain()
                    added = add(base + n_visits + (k + 1), k, code[Q + k])
                    if k < LAG_SUM - 1:
                        added.then_inc(s_added, 1)
                added.then_inc(s_summed, 1)
                dve.drain()
                dve.tensor_scalar(rden[:], acc_w[:, :, D:D + 1].rearrange("p w c -> p (w c)"), EPS_DEN, None, ALU.add)
                dve.drain()
                dve.reciprocal(rden[:], rden[:])
                dve.drain()


                def bias_relu(m):
                    cols = slice(m * TP * P, (m + 1) * TP * P)
                    dve.tensor_scalar(h_fm[:, cols], diag_t[:, cols], bias_gat[:, bass.ds(l, 1)],
                                      relu_floor[:, bass.ds(l, 1)], ALU.add, ALU.max).then_inc(s_h, 1)

                layer_end(lambda n: stand(dve, s_pick, l * PARTS + n), True, bias_relu)

            def norm(first, relu_first):
                def stats(m):
                    for n in (2 * m, 2 * m + 1):
                        _, t, k = table_tiles()[n]
                        dve.wait_ge(s_n, 2 * first + n + 1)
                        new = ps_target[n % 4][:, 0:k * D]
                        x_part = x_nm[:, t:t + k, :].rearrange("p t d -> p (t d)")
                        if relu_first:
                            dve.scalar_tensor_tensor(x_part, new, 0.0, x_part, ALU.max, ALU.add).then_inc(s_nu, 1)
                        else:
                            dve.tensor_tensor(x_part, new, x_part, ALU.add).then_inc(s_nu, 1)
                    dve.drain()
                    part = slice(m * TP, (m + 1) * TP)
                    for t in range(m * TP, (m + 1) * TP):
                        dve.bn_stats(bn6[:, t, :], x_nm[:, t, :])
                    dve.drain()
                    for t in range(m * TP, (m + 1) * TP):
                        dve.bn_aggr(mv[:, t, :], bn6[:, t, :])
                    dve.drain()
                    dve.tensor_scalar(rstd[:, part], mv[:, part, 1], EPS_LN, None, ALU.add).then_inc(s_var, 1)

                def apply(m):
                    dve.wait_ge(s_root, first + m + 1)
                    dve.reciprocal(rstd[:, m * TP:(m + 1) * TP], rstd[:, m * TP:(m + 1) * TP])
                    dve.drain()
                    for t in range(m * TP, (m + 1) * TP):
                        dve.tensor_scalar(x_nm[:, t, :], x_nm[:, t, :], mv[:, t, 0:1], rstd[:, t:t + 1],
                                          ALU.subtract, ALU.mult).then_inc(s_norm, 1)

                for m in range(PARTS):
                    stats(m)
                    if m >= 1:
                        apply(m - 1)
                apply(PARTS - 1)

            norm(0, False)
            dve.wait_ge(s_g, 1)
            dve.tensor_tensor(gz[:], ps_gate[:, 0:NT * NREL].rearrange("p (t r) -> p t r", r=NREL),
                              gbias[:].unsqueeze(1).to_broadcast([P, NT, NREL]), ALU.add).then_inc(s_gz, 1)
            dve.wait_ge(s_ge, 1)
            dve.tensor_scalar(gate[:], ge[:], 1.0, None, ALU.add)
            dve.drain()
            dve.reciprocal(gate[:], gate[:]).then_inc(s_gate, 1)

            def gated(t):
                if t >= GBUF:
                    dve.wait_ge(s_gt[t % GBUF], 16 * (t // GBUF))
                dve.tensor_tensor(gmsg[:, t % GBUF, 0:R_DVE * D].rearrange("p (r d) -> p r d", r=R_DVE),
                                  msg[:, t % 2, 0:R_DVE * D].rearrange("p (r d) -> p r d", r=R_DVE),
                                  gate[:, t, 0:R_DVE].unsqueeze(2).to_broadcast([P, R_DVE, D]),
                                  ALU.mult).then_inc(s_gd, 1)

            for t in range(NT):
                dve.wait_ge(s_m, t + 1)
                if t >= 2:
                    dve.wait_ge(s_gm, t - 1)
                for q in range(2):
                    last = dve.tensor_tensor(msg[:, t % 2, q * 512:(q + 1) * 512], ps[2 * (t % 2) + q][:],
                                             relb_bc[:, q * 512:(q + 1) * 512], ALU.add)
                last.then_inc(s_mu, 1)
                if t >= 1:
                    gated(t - 1)
                dve.drain()
            gated(NT - 1)

            dve.wait_ge(s_zero, (L + 1) * PARTS)
            base = n_visits * L

            def match(b, code):
                group = group_of(dve, code)
                rows_landed(group, L)
                d, n = members(group, window_of(dve, code), H)
                dve.tensor_tensor(lmask[:, b].rearrange("p j (h n) -> p j h n", h=H), d, n,
                                  ALU.is_equal).then_inc(s_mask, 1)

            def add_plain(t, b, code):
                dve.wait_ge(s_sum, t)
                s = acc[:, bass.ds(window_of(dve, code) * AW, D)]
                return dve.tensor_tensor(s, s, ps_sum[b][:, 0:D], ALU.add)

            code = codes(dve, ENG.DVE, 0, Q)
            for k in range(Q):
                if k >= LAG:
                    add_plain(base + (k + 1 - LAG + LAG_ADD), k % 2, code[k - LAG])
                match(k % 2, code[k])
                dve.drain()
            with dve.Fori(1, n_short) as i:
                code = codes(dve, ENG.DVE, i * Q - LAG, Q + LAG)
                for k in range(Q):
                    add_plain(base + i * Q + (k + 1 - LAG + LAG_ADD), k % 2, code[k])
                    match(k % 2, code[k + LAG])
                    dve.drain()
            code = codes(dve, ENG.DVE, tail + (Q - LAG), LAG)
            for b in range(LAG):
                added = add_plain(base + n_visits + (b + 1 - LAG + LAG_ADD), b, code[b])
                if b == LAG - 1:
                    added.then_inc(s_summed, 1)
                dve.drain()
            layer_end(lambda n: dve.wait_ge(s_pick, L * PARTS + n), False, None)
            norm(PARTS, True)


_INS = ["x", "src", "dst", "edge_type_8", "L0_gnn_Ws", "L0_gnn_Wd", "L0_gnn_att_s", "L0_gnn_att_d", "L0_gnn_b",
        "L1_gnn_W", "L1_gnn_bias_term", "L1_gnn_gate_weight", "L1_gnn_gate_bias", "L1_gnn_loop_weight"]


def kernel(**inputs):
    import numpy as _np
    import concourse.bacc as _bacc
    from concourse import mybir as _mybir
    from concourse.bass_utils import run_bass_kernel_spmd as _run

    nc = _bacc.Bacc("TRN2", target_bir_lowering=False, num_devices=1)
    arrays, args = {}, []
    for name in _INS:
        a = _np.ascontiguousarray(inputs[name])
        arrays[f"in_{name}_dram"] = a
        args.append(nc.dram_tensor(f"in_{name}_dram", a.shape, _mybir.dt.from_np(a.dtype), kind="ExternalInput").ap())
    result = nc.dram_tensor("out_0_dram", (N, D), F32, kind="ExternalOutput").ap()
    build(nc, *args, result)
    r = _run(nc, [arrays], core_ids=[0])
    return r.results[0]["out_0_dram"]
```
